# Optimizing a Trainium2 kernel written in Bass

```python
import numpy as np
import jax
import jax.numpy as jnp

def _softmax(x, axis=-1):
    return jax.nn.softmax(x, axis=axis)

def _gelu(x):
    return jax.nn.gelu(x, approximate=True)

def _silu(x):
    return jax.nn.silu(x)

def _sigmoid(x):
    return jax.nn.sigmoid(x)

def _layernorm(x, axis=-1, eps=1e-05):
    m = jnp.mean(x, axis=axis, keepdims=True)
    v = jnp.var(x, axis=axis, keepdims=True)
    return (x - m) / jnp.sqrt(v + eps)

def _scatter_add(tgt, idx, src, axis=0):
    return tgt.at[idx].add(src)

def _segment_sum(src, seg, n):
    return jax.ops.segment_sum(src, seg, n)
kernel_name = 'mk_macaron_d2_jaxref_r8_346f69'

def setup_inputs(seed: int=0):
    np.random.seed(seed)
    _w = jnp.asarray

    def _L0_attn_setup():
        import jax, jax.numpy as jnp
        import numpy as np
        import math
        DK = 128
        key = jax.random.key(seed)
        k1, k2 = jax.random.split(key)
        x = jax.random.normal(k1, (4, 256, 128), dtype=jnp.float32)
        W = jax.random.normal(k2, (128, 3 * DK), dtype=jnp.float32) * (1.0 / math.sqrt(128))
        b = jnp.zeros((3 * DK,), dtype=jnp.float32)
        return {'x': x, 'W': W, 'b': b}
    _L0_attn_in = _L0_attn_setup()

    def _L0_ffn_setup():
        import jax, jax.numpy as jnp
        import numpy as np
        D_MODEL = 128
        N_EXPERTS = 8
        TOP_K = 2
        key = jax.random.key(seed)
        ks = jax.random.split(key, 8)
        d, e = (D_MODEL, N_EXPERTS)
        s = 1.0 / np.sqrt(d)
        return {'x': jax.random.normal(ks[0], (4, 256, d), dtype=jnp.float32), 'W_gate': jax.random.uniform(ks[1], (d, e), jnp.float32, -s, s), 'b_gate': jax.random.uniform(ks[2], (e,), jnp.float32, -s, s), 'W1': jax.random.uniform(ks[3], (e, d, d), jnp.float32, -s, s), 'b1': jax.random.uniform(ks[4], (e, d), jnp.float32, -s, s), 'W2': jax.random.uniform(ks[5], (e, d, d), jnp.float32, -s, s), 'b2': jax.random.uniform(ks[6], (e, d), jnp.float32, -s, s)}
    _L0_ffn_in = _L0_ffn_setup()

    def _L1_attn_setup():
        import jax, jax.numpy as jnp
        import numpy as np
        B, S, D = (4, 512, 128)
        key = jax.random.key(seed)
        kx, kq, kk, kv, kp = jax.random.split(key, 5)
        scale = 1.0 / np.sqrt(D)
        return {'x': jax.random.normal(kx, (B, S, D), dtype=jnp.float32), 'Wq': jax.random.normal(kq, (D, D), dtype=jnp.float32) * scale, 'Wk': jax.random.normal(kk, (D, D), dtype=jnp.float32) * scale, 'Wv': jax.random.normal(kv, (D, D), dtype=jnp.float32) * scale, 'P': jax.random.normal(kp, (D, D), dtype=jnp.float32) * scale}
    _L1_attn_in = _L1_attn_setup()

    def _L1_ffn_setup():
        import jax, jax.numpy as jnp
        import numpy as np
        DIM = 128
        N_HEADS = 16
        N_KV_HEADS = 4
        HEAD_DIM = DIM // N_HEADS
        N_REP = N_HEADS // N_KV_HEADS
        N_EXPERTS = 4
        TOP_K = 2
        HIDDEN = 3 * DIM
        EPS = 1.1920928955078125e-07

        def _rmsnorm(x, g):
            var = jnp.mean(jnp.square(x), axis=-1, keepdims=True)
            return x * jax.lax.rsqrt(var + EPS) * g

        def _rotate_half(x):
            x1, x2 = jnp.split(x, 2, axis=-1)
            return jnp.concatenate([-x2, x1], axis=-1)

        def _rope_tables(S):
            inv_freq = 1.0 / 10000.0 ** (jnp.arange(0, HEAD_DIM, 2, dtype=jnp.float32) / HEAD_DIM)
            freqs = jnp.arange(S, dtype=jnp.float32)[:, None] * inv_freq[None, :]
            emb = jnp.concatenate([freqs, freqs], axis=-1)
            return (jnp.cos(emb), jnp.sin(emb))

        def _attention(x, wq, wk, wv, wo):
            B, S, D = x.shape
            q = (x @ wq).reshape(B, S, N_HEADS, HEAD_DIM).transpose(0, 2, 1, 3)
            k = (x @ wk).reshape(B, S, N_KV_HEADS, HEAD_DIM).transpose(0, 2, 1, 3)
            v = (x @ wv).reshape(B, S, N_KV_HEADS, HEAD_DIM).transpose(0, 2, 1, 3)
            cos, sin = _rope_tables(S)
            q = q * cos + _rotate_half(q) * sin
            k = k * cos + _rotate_half(k) * sin
            k = jnp.repeat(k, N_REP, axis=1)
            v = jnp.repeat(v, N_REP, axis=1)
            scores = jnp.einsum('bhqd,bhkd->bhqk', q, k) / jnp.sqrt(jnp.float32(HEAD_DIM))
            causal = jnp.tril(jnp.ones((S, S), dtype=bool))
            scores = jnp.where(causal, scores, -jnp.inf)
            attn = jax.nn.softmax(scores, axis=-1)
            out = jnp.einsum('bhqk,bhkd->bhqd', attn, v)
            return out.transpose(0, 2, 1, 3).reshape(B, S, D) @ wo

        def _moe(x, gate, w1, w2, w3):
            B, S, D = x.shape
            xf = x.reshape(-1, D)
            probs = jax.nn.softmax(xf @ gate, axis=-1)
            w, idx = jax.lax.top_k(probs, TOP_K)
            w = w / jnp.sum(w, axis=-1, keepdims=True)
            oh = jax.nn.one_hot(idx, N_EXPERTS, dtype=xf.dtype)
            comb = jnp.einsum('nk,nke->ne', w, oh)
            out = jnp.zeros_like(xf)
            for e in range(N_EXPERTS):
                h = jax.nn.silu(xf @ w1[e]) * (xf @ w3[e])
                out = out + comb[:, e:e + 1] * (h @ w2[e])
            return out.reshape(B, S, D)
        key = jax.random.key(seed)
        ks = jax.random.split(key, 12)
        s = 0.02
        B, S = (2, 256)
        return {'x': jax.random.normal(ks[0], (B, S, DIM), jnp.float32), 'g1': jnp.ones((DIM,), jnp.float32), 'g2': jnp.ones((DIM,), jnp.float32), 'wq': jax.random.normal(ks[1], (DIM, N_HEADS * HEAD_DIM), jnp.float32) * s, 'wk': jax.random.normal(ks[2], (DIM, N_KV_HEADS * HEAD_DIM), jnp.float32) * s, 'wv': jax.random.normal(ks[3], (DIM, N_KV_HEADS * HEAD_DIM), jnp.float32) * s, 'wo': jax.random.normal(ks[4], (N_HEADS * HEAD_DIM, DIM), jnp.float32) * s, 'gate': jax.random.normal(ks[5], (DIM, N_EXPERTS), jnp.float32) * s, 'w1': jax.random.normal(ks[6], (N_EXPERTS, DIM, HIDDEN), jnp.float32) * s, 'w2': jax.random.normal(ks[7], (N_EXPERTS, HIDDEN, DIM), jnp.float32) * s, 'w3': jax.random.normal(ks[8], (N_EXPERTS, DIM, HIDDEN), jnp.float32) * s}
    _L1_ffn_in = _L1_ffn_setup()
    _d = {'L0_attn_x': _L0_attn_in['x'], 'L0_attn_W': _L0_attn_in['W'], 'L0_attn_b': _L0_attn_in['b'], 'L0_ffn_W_gate': _L0_ffn_in['W_gate'], 'L0_ffn_b_gate': _L0_ffn_in['b_gate'], 'L0_ffn_W1': _L0_ffn_in['W1'], 'L0_ffn_b1': _L0_ffn_in['b1'], 'L0_ffn_W2': _L0_ffn_in['W2'], 'L0_ffn_b2': _L0_ffn_in['b2'], 'L1_attn_Wq': _L1_attn_in['Wq'], 'L1_attn_Wk': _L1_attn_in['Wk'], 'L1_attn_Wv': _L1_attn_in['Wv'], 'L1_attn_P': _L1_attn_in['P'], 'L1_ffn_g1': _L1_ffn_in['g1'], 'L1_ffn_g2': _L1_ffn_in['g2'], 'L1_ffn_wq': _L1_ffn_in['wq'], 'L1_ffn_wk': _L1_ffn_in['wk'], 'L1_ffn_wv': _L1_ffn_in['wv'], 'L1_ffn_wo': _L1_ffn_in['wo'], 'L1_ffn_gate': _L1_ffn_in['gate'], 'L1_ffn_w1': _L1_ffn_in['w1'], 'L1_ffn_w2': _L1_ffn_in['w2'], 'L1_ffn_w3': _L1_ffn_in['w3']}
    _x0 = _d['L0_attn_x']
    _d['L0_attn_x'] = jax.random.normal(jax.random.fold_in(jax.random.key(seed), 1), (16, 512, 128), dtype=_x0.dtype)
    del _x0
    return _d

def reference(L0_attn_x, L0_attn_W, L0_attn_b, L0_ffn_W_gate, L0_ffn_b_gate, L0_ffn_W1, L0_ffn_b1, L0_ffn_W2, L0_ffn_b2, L1_attn_Wq, L1_attn_Wk, L1_attn_Wv, L1_attn_P, L1_ffn_g1, L1_ffn_g2, L1_ffn_wq, L1_ffn_wk, L1_ffn_wv, L1_ffn_wo, L1_ffn_gate, L1_ffn_w1, L1_ffn_w2, L1_ffn_w3):

    def _L0_attn_ref(x, W, b):
        import jax, jax.numpy as jnp
        import numpy as np
        import math
        DK = 128
        qkv = jnp.einsum('btc,cd->btd', x, W) + b
        q, k, v = jnp.split(qkv, 3, axis=-1)
        scale = 1.0 / math.sqrt(DK)
        weights = jnp.einsum('btc,bTc->btT', q, k) * scale
        T = weights.shape[-1]
        mask = jnp.tril(jnp.ones((T, T), dtype=jnp.float32))
        logits = jnp.where(mask == 0, jnp.float32(-9000000000000000.0), weights)
        attention = jax.nn.softmax(logits, axis=-1)
        values = jnp.einsum('btT,bTc->btc', attention, v)
        return values

    def _L0_ffn_ref(x, W_gate, b_gate, W1, b1, W2, b2):
        import jax, jax.numpy as jnp
        import numpy as np
        D_MODEL = 128
        N_EXPERTS = 8
        TOP_K = 2
        B, T, d = x.shape
        xf = x.reshape(-1, d)
        scores = xf @ W_gate + b_gate
        topk_val, topk_idx = jax.lax.top_k(scores, TOP_K)
        onehot = jax.nn.one_hot(topk_idx, N_EXPERTS, dtype=xf.dtype)
        w = jnp.einsum('nk,nke->ne', topk_val, onehot)
        h = jax.nn.relu(jnp.einsum('nd,edh->neh', xf, W1) + b1)
        y = jnp.einsum('neh,ehd->ned', h, W2) + b2
        out = jnp.einsum('ned,ne->nd', y, w)
        return out.reshape(B, T, d)

    def _L1_attn_ref(x, Wq, Wk, Wv, P):
        import jax, jax.numpy as jnp
        import numpy as np
        B, S, D = (4, 512, 128)
        Q = jnp.einsum('bsd,dk->bsk', x, Wq)
        K = jnp.einsum('bsd,dk->bsk', x, Wk)
        V = jnp.einsum('bsd,dv->bsv', x, Wv)
        scores = jnp.einsum('bsk,btk->bst', Q, K)
        context = jnp.einsum('bst,btv->bsv', scores, V)
        return x + jnp.einsum('bsv,vo->bso', context, P)

    def _L1_ffn_ref(x, g1, g2, wq, wk, wv, wo, gate, w1, w2, w3):
        import jax, jax.numpy as jnp
        import numpy as np
        DIM = 128
        N_HEADS = 16
        N_KV_HEADS = 4
        HEAD_DIM = DIM // N_HEADS
        N_REP = N_HEADS // N_KV_HEADS
        N_EXPERTS = 4
        TOP_K = 2
        HIDDEN = 3 * DIM
        EPS = 1.1920928955078125e-07

        def _rmsnorm(x, g):
            var = jnp.mean(jnp.square(x), axis=-1, keepdims=True)
            return x * jax.lax.rsqrt(var + EPS) * g

        def _rotate_half(x):
            x1, x2 = jnp.split(x, 2, axis=-1)
            return jnp.concatenate([-x2, x1], axis=-1)

        def _rope_tables(S):
            inv_freq = 1.0 / 10000.0 ** (jnp.arange(0, HEAD_DIM, 2, dtype=jnp.float32) / HEAD_DIM)
            freqs = jnp.arange(S, dtype=jnp.float32)[:, None] * inv_freq[None, :]
            emb = jnp.concatenate([freqs, freqs], axis=-1)
            return (jnp.cos(emb), jnp.sin(emb))

        def _attention(x, wq, wk, wv, wo):
            B, S, D = x.shape
            q = (x @ wq).reshape(B, S, N_HEADS, HEAD_DIM).transpose(0, 2, 1, 3)
            k = (x @ wk).reshape(B, S, N_KV_HEADS, HEAD_DIM).transpose(0, 2, 1, 3)
            v = (x @ wv).reshape(B, S, N_KV_HEADS, HEAD_DIM).transpose(0, 2, 1, 3)
            cos, sin = _rope_tables(S)
            q = q * cos + _rotate_half(q) * sin
            k = k * cos + _rotate_half(k) * sin
            k = jnp.repeat(k, N_REP, axis=1)
            v = jnp.repeat(v, N_REP, axis=1)
            scores = jnp.einsum('bhqd,bhkd->bhqk', q, k) / jnp.sqrt(jnp.float32(HEAD_DIM))
            causal = jnp.tril(jnp.ones((S, S), dtype=bool))
            scores = jnp.where(causal, scores, -jnp.inf)
            attn = jax.nn.softmax(scores, axis=-1)
            out = jnp.einsum('bhqk,bhkd->bhqd', attn, v)
            return out.transpose(0, 2, 1, 3).reshape(B, S, D) @ wo

        def _moe(x, gate, w1, w2, w3):
            B, S, D = x.shape
            xf = x.reshape(-1, D)
            probs = jax.nn.softmax(xf @ gate, axis=-1)
            w, idx = jax.lax.top_k(probs, TOP_K)
            w = w / jnp.sum(w, axis=-1, keepdims=True)
            oh = jax.nn.one_hot(idx, N_EXPERTS, dtype=xf.dtype)
            comb = jnp.einsum('nk,nke->ne', w, oh)
            out = jnp.zeros_like(xf)
            for e in range(N_EXPERTS):
                h = jax.nn.silu(xf @ w1[e]) * (xf @ w3[e])
                out = out + comb[:, e:e + 1] * (h @ w2[e])
            return out.reshape(B, S, D)
        x = x + _attention(_rmsnorm(x, g1), wq, wk, wv, wo)
        x = x + _moe(_rmsnorm(x, g2), gate, w1, w2, w3)
        return x
    x = L0_attn_x
    x = x + 0.5 * _L0_ffn_ref(_layernorm(x, axis=-1), L0_ffn_W_gate, L0_ffn_b_gate, L0_ffn_W1, L0_ffn_b1, L0_ffn_W2, L0_ffn_b2)
    x = x + _L0_attn_ref(_layernorm(x, axis=-1), L0_attn_W, L0_attn_b)
    x = x + 0.5 * _L0_ffn_ref(_layernorm(x, axis=-1), L0_ffn_W_gate, L0_ffn_b_gate, L0_ffn_W1, L0_ffn_b1, L0_ffn_W2, L0_ffn_b2)
    x = x + 0.5 * _L1_ffn_ref(_layernorm(x, axis=-1), L1_ffn_g1, L1_ffn_g2, L1_ffn_wq, L1_ffn_wk, L1_ffn_wv, L1_ffn_wo, L1_ffn_gate, L1_ffn_w1, L1_ffn_w2, L1_ffn_w3)
    x = x + _L1_attn_ref(_layernorm(x, axis=-1), L1_attn_Wq, L1_attn_Wk, L1_attn_Wv, L1_attn_P)
    x = x + 0.5 * _L1_ffn_ref(_layernorm(x, axis=-1), L1_ffn_g1, L1_ffn_g2, L1_ffn_wq, L1_ffn_wk, L1_ffn_wv, L1_ffn_wo, L1_ffn_gate, L1_ffn_w1, L1_ffn_w2, L1_ffn_w3)
    return x

_drawn_inputs = setup_inputs


def setup_inputs(seed=0):
    import zlib

    import numpy as np

    out = dict(_drawn_inputs(seed))
    spreads = {'L0_attn_b': (0.0, 0.1), 'L1_ffn_g1': (1.0, 0.6), 'L1_ffn_g2': (1.0, 0.6)}
    factors = {'L1_ffn_wq': 8.0,
     'L1_ffn_wk': 8.0,
     'L1_ffn_wv': 8.0,
     'L1_ffn_wo': 8.0,
     'L1_ffn_gate': 8.0,
     'L1_ffn_w1': 8.0,
     'L1_ffn_w2': 8.0,
     'L1_ffn_w3': 8.0}
    for name, (base, spread) in spreads.items():
        noise = np.random.default_rng([zlib.crc32(name.encode()), seed]).standard_normal(out[name].shape)
        drawn = base * np.exp(spread * noise) if base else spread * noise
        out[name] = jnp.asarray(drawn.astype(out[name].dtype))
    for name, factor in factors.items():
        out[name] = (out[name] * factor).astype(out[name].dtype)
    return out
```

```python
from contextlib import ExitStack

import concourse.bass as bass
from concourse import mybir

F32 = mybir.dt.float32
BF16 = mybir.dt.bfloat16
ALU = mybir.AluOpType
ACT = mybir.ActivationFunctionType
AX_X = mybir.AxisListType.X

DVE_OWN, POOL_OWN = 94, 44
P = 128
LN_EPS = 1e-5
RMS_EPS = 1.1920928955078125e-07
MASKED = -1.0e30
TAKEN = -3.0e38


class Rises:

    def __init__(self, sem, per_turn):
        self.sem, self.per_turn, self.seen = sem, per_turn, 0

    def at(self, turn, n):
        return turn * self.per_turn + n


def macaron_kernel(nc, ins, out):
    x_dram = ins["x"]
    B, S, D = x_dram.shape
    T = S // P
    NE0 = ins["W1"].shape[0]
    NE1, _, HID = ins["w1"].shape
    CH = HID // P
    NU = NE1 * CH
    H, KV = 16, 4
    REP = H // KV
    HD = D // H
    PART = 3
    ROWS = PART * PART * HD
    QK = ROWS + PART
    assert D == P and T == 4 and HD == 8 and REP == 4 and CH == 3

    NORMS, FFNS, MHAS, MOES = 8, 2, 2, 2
    NSTACK = 2 * PART * PART
    MXU, TU = 6, 10

    with ExitStack() as ctx:
        def sb(name, shape, dt=F32):
            return ctx.enter_context(nc.sbuf_tensor(name, shape, dt))

        def rises(name, per_turn):
            return Rises(ctx.enter_context(nc.semaphore(name)), per_turn)

        bank = ctx.enter_context(nc.psum_tensor("bank", [P, 8, 512], F32))

        ident = sb("ident", [P, P])
        identb = sb("identb", [P, P], BF16)
        causal = sb("causal", [P, P])
        causalb = sb("causalb", [P, P], BF16)
        rank = sb("rank", [P, T, NE0])
        minus_half = sb("minus_half", [P, T])
        cosq = sb("cosq", [P, S])
        sinq = sb("sinq", [P, S])
        cossink = sb("cossink", [2 * HD * KV, S])
        Wg = sb("Wg", [P, NE0])
        bg = sb("bg", [P, NE0])
        W1 = sb("W1", [P, NE0, P])
        b1 = sb("b1", [P, NE0])
        W2 = sb("W2", [P, NE0, P])
        b2 = sb("b2", [NE0, P])
        Wqkv = sb("Wqkv", [P, 3 * P])
        bqk = sb("bqk", [P, 2])
        bv = sb("bv", [P, P])
        WqT = sb("WqT", [P, P])
        WkT = sb("WkT", [P, P])
        WvT = sb("WvT", [P, P])
        Wp = sb("Wp", [P, P])
        AT = sb("AT", [P, P])
        C = sb("C", [P, P])
        g = sb("g", [P, 2])
        mproj = sb("mproj", [P, 2 * P + 3 * HD * KV])
        wo = sb("wo", [P, P])
        gate = sb("gate", [P, NE1])
        w13 = sb("w13", [P, 2, NE1, HID])
        w2 = sb("w2", [P, NE1, CH, P])
        w_q, w_qs = mproj[:, 0:P], mproj[:, P:2 * P]
        w_kk = mproj[:, 2 * P:2 * P + 2 * HD * KV]
        w_v = mproj[:, 2 * P + 2 * HD * KV:]

        Xin = sb("Xin", [P, T, P])
        X = sb("X", [P, T, P])
        XN = sb("XN", [P, T, P])
        XR = sb("XR", [P, T, P])
        Y = sb("Y", [P, T, P])
        xT = sb("xT", [P, S])
        stats = sb("stats", [P, T, 6])
        mv = sb("mv", [P, T, 2])
        var_eps = sb("var_eps", [P, T])
        rstd = sb("rstd", [P, T])
        rsq = sb("rsq", [P, T])
        rms_in = sb("rms_in", [P, T])
        rms = sb("rms", [P, T])

        score = sb("score", [P, T, NE0])
        score2 = sb("score2", [P, T, NE0])
        top = sb("top", [P, 4, T])
        tie = sb("tie", [P, 2, T, NE0])
        hot = sb("hot", [P, 3, T, NE0])
        escore = sb("escore", [P, T, NE1])
        epick = sb("epick", [P, T, NE1])
        esum = sb("esum", [P, 2, T])
        wroute = sb("wroute", [P, T, NE0])
        wrouteT = sb("wrouteT", [NE0, S])

        hT = sb("hT", [P, 2, S])
        gT = sb("gT", [P, 2, S])

        qT = sb("qT", [P, S])
        kT = sb("kT", [P, S])
        V = sb("V", [P, T, P])
        neg_max = sb("neg_max", [P, T])
        neg_bias = sb("neg_bias", [P, T])
        probs = sb("probs", [P, 2, S])
        probsT = sb("probsT", [P, 2, S])
        row_sum = sb("row_sum", [P, T])
        row_rec = sb("row_rec", [P, T])

        gram = sb("gram", [P, P])
        gramC = sb("gramC", [P, P])
        mix = sb("mix", [P, P])

        rope_a = sb("rope_a", [P, S])
        rope_b = sb("rope_b", [P, S])
        rope_ka = sb("rope_ka", [HD * KV, S])
        rope_kb = sb("rope_kb", [HD * KV, S])
        q_rest = sb("q_rest", [P, S])
        k_rest = sb("k_rest", [HD * KV, S])
        q_part = sb("q_part", [P, PART, S], BF16)
        k_part = sb("k_part", [HD * KV, PART, S], BF16)
        Qs = sb("Qs", [QK, H, S], BF16)
        Ks = sb("Ks", [QK, KV, S], BF16)
        Vp = sb("Vp", [P, T, KV, 32])
        nmax = sb("nmax", [P, REP, T])
        nrest = sb("nrest", [P, REP, T])
        nparts = sb("nparts", [P, 2, T, PART, REP], BF16)
        nmaxT = sb("nmaxT", [PART * REP, 2, S], BF16)
        RING = 6
        E = sb("E", [P, RING, S])
        OT = sb("OT", [P, 2, S])
        den = sb("den", [P, T, REP])
        heads_out = sb("heads_out", [P, T, H, HD])
        aT = sb("aT", [P, S])

        loaded = rises("loaded", 0)
        const_ready = rises("const_ready", 0)
        cleared = rises("cleared", 0)
        fold_pe = rises("fold_pe", 0)
        fold_ready = rises("fold_ready", 0)
        x_loaded = rises("x_loaded", 16)
        x_free = rises("x_free", 16)
        stats_ready = rises("stats_ready", NORMS)
        rstd_ready = rises("rstd_ready", NORMS)
        normed = rises("normed", NORMS)
        turned = rises("turned", NORMS)
        xT_ready = rises("xT_ready", NORMS)
        gate_ready = rises("gate_ready", FFNS)
        route_ready = rises("route_ready", FFNS)
        routeT_turned = rises("routeT_turned", FFNS)
        routeT_ready = rises("routeT_ready", FFNS)
        z_ready = rises("z_ready", FFNS * NE0)
        h_ready = rises("h_ready", FFNS * NE0)
        y_ready = rises("y_ready", FFNS * (NE0 + 1))
        y_used = rises("y_used", FFNS * (NE0 + 1) * T)
        mgate_ready = rises("mgate_ready", MOES)
        mshift_ready = rises("mshift_ready", MOES)
        mexp_ready = rises("mexp_ready", MOES)
        up_ready = rises("up_ready", MOES * NU)
        gated_ready = rises("gated_ready", MOES * NU)
        silu_ready = rises("silu_ready", MOES * NU)
        g_ready = rises("g_ready", MOES * NU)
        down_ready = rises("down_ready", MOES * NE1)
        down_used = rises("down_used", MOES * NE1 * T)
        qkv_ready = rises("qkv_ready", 3)
        qk_saved = rises("qk_saved", 2)
        v_saved = rises("v_saved", 1)
        s_ready = rises("s_ready", T)
        bias_ready = rises("bias_ready", T)
        p_ready = rises("p_ready", T)
        p_turned = rises("p_turned", T)
        pT_ready = rises("pT_ready", T)
        o_ready = rises("o_ready", T)
        lin_ready = rises("lin_ready", 4)
        lin_saved = rises("lin_saved", 3)
        proj_ready = rises("proj_ready", MHAS * 4)
        rope_ready = rises("rope_ready", MHAS * 2)
        part0_ready = rises("part0_ready", MHAS * 2)
        rest_ready = rises("rest_ready", MHAS * 2)
        part1_ready = rises("part1_ready", MHAS * 2)
        part2_ready = rises("part2_ready", MHAS * 2)
        vp_ready = rises("vp_ready", MHAS)
        stacked = rises("stacked", MHAS * NSTACK * 16)
        mx_ready = rises("mx_ready", MHAS * KV * MXU)
        mx_used = rises("mx_used", MHAS * KV * MXU)
        nparts_ready = rises("nparts_ready", MHAS * KV)
        nmax_turned = rises("nmax_turned", MHAS * KV)
        nmaxT_ready = rises("nmaxT_ready", MHAS * KV)
        nmax_stacked = rises("nmax_stacked", MHAS * KV * 16)
        t_ready = rises("t_ready", MHAS * KV * TU)
        e_ready = rises("e_ready", MHAS * KV * TU)
        e_masked = rises("e_masked", MHAS * KV * TU)
        av_done = rises("av_done", MHAS * KV * TU)
        ot_ready = rises("ot_ready", MHAS * KV)
        o_turned = rises("o_turned", MHAS * KV)
        heads_ready = rises("heads_ready", MHAS * KV)
        a_turned = rises("a_turned", MHAS)
        aT_ready = rises("aT_ready", MHAS)
        attn_ready = rises("attn_ready", MHAS)
        y_res_ready = rises("y_res_ready", MHAS)
        dve_own = rises("dve_own", DVE_OWN)
        pool_own = rises("pool_own", POOL_OWN)

        x_v = x_dram.rearrange("b (t p) d -> b p t d", p=P)
        out_v = out.rearrange("b (t p) d -> b p t d", p=P)

        loads = [
            (ident[:, :], ins["ident"]), (causal[:, :], ins["causal"]), (cosq[:, :], ins["cosq"]),
            (sinq[:, :], ins["sinq"]), (cossink[:, :], ins["cossink"]),
            (rank[:, :, :], ins["rank"]),
            (Wg[:, :], ins["W_gate"]), (bg[:, :], ins["b_gate"].partition_broadcast(P)),
            (W1[:, :, :], ins["W1"].rearrange("e d h -> d e h")), (b1[:, :], ins["b1T"]),
            (W2[:, :, :], ins["W2"].rearrange("e d h -> d e h")), (b2[:, :], ins["b2"]),
            (Wqkv[:, :], ins["W"]), (bqk[:, :], ins["bqk"]), (bv[:, :], ins["bv"].partition_broadcast(P)),
            (WqT[:, :], ins["WqT"]), (WkT[:, :], ins["WkT"]), (WvT[:, :], ins["WvT"]), (Wp[:, :], ins["P"]),
            (g[:, 0:1], ins["g1"]), (g[:, 1:2], ins["g2"]),
            (w_q, ins["wq"]), (w_qs, ins["wq_swap"]), (w_kk[:, 0:HD * KV], ins["wk"]),
            (w_kk[:, HD * KV:], ins["wk_swap"]), (w_v, ins["wv"]), (wo[:, :], ins["wo"]),
            (gate[:, :], ins["gate"]), (w13[:, 0, :, :], ins["w1"].rearrange("e d h -> d e h")),
            (w13[:, 1, :, :], ins["w3"].rearrange("e d h -> d e h")),
            (w2[:, :, :, :], ins["w2"].rearrange("e (c p) d -> p e c d", p=P)),
        ]

        T_UNITS = []
        for a in (0, 2):
            T_UNITS += [("first", a), ("first", a + 1), ("third", a), ("rest", a), ("rest", a + 1)]
        assert len(T_UNITS) == TU

        def pieces(unit):
            kind, a = unit
            if kind == "first":
                return [(0, a, 0, 0)]
            if kind == "third":
                return [(0, a, 2, 2), (2 * P, a + 1, 2, 2)]
            return [(0, a, 3, 3), (P, a, 1, 1)]

        block = ctx.enter_context(nc.Block())

        @block.sync
        def _(sp):
            for dst, src in loads:
                sp.dma_start(dst, src).then_inc(loaded.sem, 16)
            sp.dma_start(Xin[:, :, :], x_v[0]).then_inc(x_loaded.sem, 16)

            def turn(b, last):
                for m in range(MHAS):
                    for a, ready in enumerate((part0_ready, part1_ready, part2_ready)):
                        sp.wait_ge(ready.sem, ready.at(b, 2 * m + 2))
                        for c in range(PART):
                            r = (a * PART + c) * HD
                            sp.dma_start(Qs[r:r + HD, :, :], q_part[:, a, :]).then_inc(stacked.sem, 16)
                        for c in range(PART):
                            r = (c * PART + a) * HD
                            sp.dma_start(Ks[r:r + HD, :, :], k_part[:, a, :]).then_inc(stacked.sem, 16)
                    for hg in range(KV):
                        sp.wait_ge(nmaxT_ready.sem, nmaxT_ready.at(b, m * KV + hg + 1))
                        sp.dma_start(Qs[ROWS:QK, hg * REP:(hg + 1) * REP, :],
                                     nmaxT[:, hg % 2, :]).then_inc(nmax_stacked.sem, 16)
                    if m == 0 and not last:
                        sp.wait_ge(y_used.sem, y_used.at(b, T))
                        sp.dma_start(Xin[:, :, :], x_v[b + 1]).then_inc(x_loaded.sem, 16)
                sp.wait_ge(down_used.sem, down_used.at(b, MOES * NE1 * T))
                sp.dma_start(out_v[b], X[:, :, :]).then_inc(x_free.sem, 16)

            with sp.Fori(0, B - 1) as b:
                turn(b, False)
            turn(B - 1, True)
            sp.wait_ge(x_free.sem, 16 * (B + 1))

        @block.tensor
        def _(pe):
            mm = nc.tensor.matmul

            def tr4(dst_bank, src, last_sem):
                for t in range(T):
                    i = nc.tensor.transpose(bank[:, dst_bank, t * P:(t + 1) * P], src[:, t, :], ident[:, :])
                i.then_inc(last_sem.sem, 1)

            pe.wait_ge(loaded.sem, 16 * len(loads))
            pe.wait_ge(const_ready.sem, 1)
            mm(bank[:, 0, 0:P], WkT[:, :], WqT[:, :], start=True, stop=True)
            mm(bank[:, 1, 0:P], WvT[:, :], Wp[:, :], start=True, stop=True).then_inc(fold_pe.sem, 1)
            pe.wait_ge(fold_ready.sem, 2)

            def norm_turn(b, f, src):
                pe.wait_ge(normed.sem, normed.at(b, f + 1))
                tr4(7, src, turned)
                pe.wait_ge(xT_ready.sem, xT_ready.at(b, f + 1))

            def ffn(b, n):
                for t in range(T):
                    i = mm(bank[:, 4, t * NE0:(t + 1) * NE0], xT[:, t * P:(t + 1) * P], Wg[:, :],
                           start=True, stop=True)
                i.then_inc(gate_ready.sem, 1)

                def down(e):
                    o = n * NE0 + e
                    pe.wait_ge(h_ready.sem, h_ready.at(b, o + 1))
                    if e >= 2:
                        pe.wait_ge(y_used.sem, y_used.at(b, (n * (NE0 + 1) + e - 1) * T))
                    for t in range(T):
                        i = mm(bank[:, 2 + e % 2, t * P:(t + 1) * P], hT[:, e % 2, t * P:(t + 1) * P],
                               W2[:, e, :], start=True, stop=True)
                    i.then_inc(y_ready.sem, 1)

                for e in range(NE0):
                    if e >= 2:
                        pe.wait_ge(h_ready.sem, h_ready.at(b, n * NE0 + e - 1))
                    mm(bank[:, e % 2, :], W1[:, e, :], xT[:, :], start=True, stop=True).then_inc(z_ready.sem, 1)
                    if e >= 1:
                        down(e - 1)
                down(NE0 - 1)
                pe.wait_ge(route_ready.sem, route_ready.at(b, n + 1))
                for t in range(T):
                    i = nc.tensor.transpose(bank[0:NE0, 5, t * P:(t + 1) * P], wroute[:, t, :], ident[:, :])
                i.then_inc(routeT_turned.sem, 1)
                pe.wait_ge(routeT_ready.sem, routeT_ready.at(b, n + 1))
                pe.wait_ge(y_used.sem, y_used.at(b, (n * (NE0 + 1) + NE0 - 1) * T))
                for t in range(T):
                    i = mm(bank[:, 2, t * P:(t + 1) * P], wrouteT[:, t * P:(t + 1) * P], b2[:, :],
                           start=True, stop=True)
                i.then_inc(y_ready.sem, 1)

            def attn0(b):
                mm(bank[:, 0, :], Wqkv[:, 0:P], xT[:, :], start=True, stop=True).then_inc(qkv_ready.sem, 1)
                mm(bank[:, 1, :], Wqkv[:, P:2 * P], xT[:, :], start=True, stop=True).then_inc(qkv_ready.sem, 1)
                for t in range(T):
                    i = mm(bank[:, 2, t * P:(t + 1) * P], xT[:, t * P:(t + 1) * P], Wqkv[:, 2 * P:],
                           start=True, stop=True)
                i.then_inc(qkv_ready.sem, 1)
                pe.wait_ge(qk_saved.sem, qk_saved.at(b, 2))

                def turn_probs(t):
                    pe.wait_ge(p_ready.sem, p_ready.at(b, t + 1))
                    if t >= 2:
                        pe.wait_ge(pT_ready.sem, pT_ready.at(b, t - 1))
                    for j in range(t + 1):
                        i = nc.tensor.transpose(bank[:, 5 + t % 2, j * P:(j + 1) * P],
                                                probs[:, t % 2, j * P:(j + 1) * P], ident[:, :])
                    i.then_inc(p_turned.sem, 1)

                def values(t):
                    pe.wait_ge(pT_ready.sem, pT_ready.at(b, t + 1))
                    pe.wait_ge(v_saved.sem, v_saved.at(b, 1))
                    for j in range(t + 1):
                        i = mm(bank[:, 7, t * P:(t + 1) * P], probsT[:, t % 2, j * P:(j + 1) * P], V[:, j, :],
                               start=(t == 0 and j == 0), stop=(j == t), skip_group_check=True)
                    i.then_inc(o_ready.sem, 1)

                for t in range(T):
                    if t >= 2:
                        pe.wait_ge(p_ready.sem, p_ready.at(b, t - 1))
                    w = (t + 1) * P
                    mm(bank[:, 3 + t % 2, 0:w], qT[:, t * P:(t + 1) * P], kT[:, 0:w], start=True, stop=True)
                    mm(bank[:, 3 + t % 2, t * P:w], identb[:, :], causalb[:, :], start=False, stop=True,
                       skip_group_check=True).then_inc(s_ready.sem, 1)
                    if t >= 1:
                        turn_probs(t - 1)
                    if t >= 2:
                        values(t - 2)
                turn_probs(T - 1)
                values(T - 2)
                values(T - 1)

            def linear(b):
                for t in range(T):
                    i = mm(bank[:, 0, 0:P], XN[:, t, :], XN[:, t, :], start=(t == 0), stop=(t == T - 1))
                i.then_inc(lin_ready.sem, 1)
                pe.wait_ge(lin_saved.sem, lin_saved.at(b, 1))
                mm(bank[:, 1, 0:P], gram[:, :], C[:, :], start=True, stop=True).then_inc(lin_ready.sem, 1)
                pe.wait_ge(lin_saved.sem, lin_saved.at(b, 2))
                mm(bank[:, 2, 0:P], AT[:, :], gramC[:, :], start=True, stop=True).then_inc(lin_ready.sem, 1)
                pe.wait_ge(lin_saved.sem, lin_saved.at(b, 3))
                for t in range(T):
                    i = mm(bank[:, 3, t * P:(t + 1) * P], xT[:, t * P:(t + 1) * P], mix[:, :],
                           start=True, stop=True)
                i.then_inc(lin_ready.sem, 1)

            def mha(b, m):
                mm(bank[:, 0, :], w_q, xT[:, :], start=True, stop=True).then_inc(proj_ready.sem, 1)
                mm(bank[:, 1, :], w_qs, xT[:, :], start=True, stop=True).then_inc(proj_ready.sem, 1)
                mm(bank[0:2 * HD * KV, 2, :], w_kk, xT[:, :], start=True, stop=True).then_inc(proj_ready.sem, 1)
                for t in range(T):
                    i = mm(bank[:, 3, t * HD * KV:(t + 1) * HD * KV], xT[:, t * P:(t + 1) * P], w_v,
                           start=True, stop=True)
                i.then_inc(proj_ready.sem, 1)
                pe.wait_ge(stacked.sem, stacked.at(b, (m + 1) * NSTACK * 16))
                pe.wait_ge(vp_ready.sem, vp_ready.at(b, m + 1))

                def mx_piece(hg, j, t, bk, col):
                    h, w = hg * REP + j, (t + 1) * P
                    mm(bank[:, bk, col:col + w], Qs[0:ROWS, h, t * P:w], Ks[0:ROWS, hg, 0:w],
                       start=True, stop=True)
                    return mm(bank[:, bk, col + t * P:col + w], identb[:, :], causalb[:, :],
                              start=False, stop=True, skip_group_check=True)

                def mx_unit(hg, u):
                    n = (m * KV + hg) * MXU + u
                    if hg * MXU + u >= 2:
                        pe.wait_ge(mx_used.sem, mx_used.at(b, n - 1))
                    b0 = 2 * (u % 2)
                    if u < 2:
                        for j in range(2):
                            i = mx_piece(hg, 2 * u + j, 3, b0 + j, 0)
                    elif u < 4:
                        for j in range(2):
                            i = mx_piece(hg, 2 * (u - 2) + j, 2, b0 + j, 0)
                    elif u == 4:
                        for j in range(4):
                            i = mx_piece(hg, j, 1, b0 + j // 2, (j % 2) * 2 * P)
                    else:
                        for j in range(4):
                            i = mx_piece(hg, j, 0, b0, j * P)
                    i.then_inc(mx_ready.sem, 1)

                def nmax_turn(hg):
                    pe.wait_ge(nparts_ready.sem, nparts_ready.at(b, m * KV + hg + 1))
                    if hg:
                        pe.wait_ge(nmaxT_ready.sem, nmaxT_ready.at(b, m * KV + hg))
                    bb = bank[:, 7, :].bitcast(BF16)
                    for t in range(T):
                        i = nc.tensor.transpose(bb[0:PART * REP, t * P:(t + 1) * P],
                                                nparts[:, hg % 2, t, :, :].rearrange("p a j -> p (a j)"),
                                                identb[:, :])
                    i.then_inc(nmax_turned.sem, 1)

                def t_unit(hg, u):
                    n = (m * KV + hg) * TU + u
                    if hg * TU + u >= 2:
                        pe.wait_ge(e_ready.sem, e_ready.at(b, n - 1))
                    for col, j, kt, q0 in pieces(T_UNITS[u]):
                        i = mm(bank[:, 4 + n % 2, col:col + (T - q0) * P], Ks[:, hg, kt * P:(kt + 1) * P],
                               Qs[:, hg * REP + j, q0 * P:], start=True, stop=True)
                    i.then_inc(t_ready.sem, 1)

                def av_unit(hg, u):
                    n = (m * KV + hg) * TU + u
                    pe.wait_ge(e_masked.sem, e_masked.at(b, n + 1))
                    if u == 0 and hg:
                        pe.wait_ge(ot_ready.sem, ot_ready.at(b, m * KV + hg))
                    for col, j, kt, q0 in pieces(T_UNITS[u]):
                        i = mm(bank[32 * j:32 * j + 32, 6, q0 * P:], Vp[:, kt, hg, :],
                               E[:, n % RING, col:col + (T - q0) * P],
                               start=(kt == 0), stop=True, skip_group_check=True)
                    i.then_inc(av_done.sem, 1)

                def o_turn(hg):
                    pe.wait_ge(ot_ready.sem, ot_ready.at(b, m * KV + hg + 1))
                    pe.wait_ge(nmaxT_ready.sem, nmaxT_ready.at(b, m * KV + min(hg + 2, KV)))
                    if hg:
                        pe.wait_ge(heads_ready.sem, heads_ready.at(b, m * KV + hg))
                    tr4(7, OT[:, hg % 2, :].rearrange("p (t q) -> p t q", t=T), o_turned)

                for step in range(KV + 1):
                    mx_at = [0, 1, 3, 5, 7, 8]
                    if step >= 2:
                        pass
                    for k in range(TU + 2):
                        if step < KV and k in mx_at:
                            mx_unit(step, mx_at.index(k))
                        if step >= 1 and k < TU:
                            if k == 0:
                                pe.wait_ge(nmax_stacked.sem, nmax_stacked.at(b, (m * KV + step) * 16))
                            t_unit(step - 1, k)
                        if step >= 1 and k >= 2:
                            av_unit(step - 1, k - 2)
                    if step < KV:
                        nmax_turn(step)
                    if step >= 1:
                        o_turn(step - 1)
                        if step < KV:
                            pe.wait_ge(heads_ready.sem, heads_ready.at(b, m * KV + step))

                pe.wait_ge(heads_ready.sem, heads_ready.at(b, (m + 1) * KV))
                tr4(7, heads_out[:, :, :, :].rearrange("p t h d -> p t (h d)"), a_turned)
                pe.wait_ge(aT_ready.sem, aT_ready.at(b, m + 1))
                for t in range(T):
                    i = mm(bank[:, 6, t * P:(t + 1) * P], aT[:, t * P:(t + 1) * P], wo[:, :],
                           start=True, stop=True)
                i.then_inc(attn_ready.sem, 1)

            def moe(b, n):
                for t in range(T):
                    i = mm(bank[:, 4, t * NE1:(t + 1) * NE1], xT[:, t * P:(t + 1) * P], gate[:, :],
                           start=True, stop=True)
                i.then_inc(mgate_ready.sem, 1)

                def down(u):
                    e, c = divmod(u, CH)
                    pe.wait_ge(g_ready.sem, g_ready.at(b, n * NU + u + 1))
                    if c == 0 and e >= 2:
                        pe.wait_ge(down_used.sem, down_used.at(b, (n * NE1 + e - 1) * T))
                    for t in range(T):
                        i = mm(bank[:, 2 + e % 2, t * P:(t + 1) * P], gT[:, u % 2, t * P:(t + 1) * P],
                               w2[:, e, c, :], start=(c == 0 and t == 0), stop=(c == CH - 1),
                               skip_group_check=True)
                    if c == CH - 1:
                        i.then_inc(down_ready.sem, 1)

                for u in range(NU):
                    e, c = divmod(u, CH)
                    if u:
                        pe.wait_ge(silu_ready.sem, silu_ready.at(b, n * NU + u))
                    mm(bank[:, 0, :], w13[:, 0, e, c * P:(c + 1) * P], xT[:, :], start=True, stop=True)\
                        .then_inc(gated_ready.sem, 1)
                    if u:
                        pe.wait_ge(g_ready.sem, g_ready.at(b, n * NU + u))
                    mm(bank[:, 1, :], w13[:, 1, e, c * P:(c + 1) * P], xT[:, :], start=True, stop=True)\
                        .then_inc(up_ready.sem, 1)
                    if u:
                        down(u - 1)
                down(NU - 1)

            with pe.Fori(0, B) as b:
                norm_turn(b, 0, XN)
                ffn(b, 0)
                norm_turn(b, 1, XN)
                attn0(b)
                norm_turn(b, 2, XN)
                ffn(b, 1)
                norm_turn(b, 3, XR)
                mha(b, 0)
                norm_turn(b, 4, XR)
                moe(b, 0)
                norm_turn(b, 5, XN)
                linear(b)
                norm_turn(b, 6, XR)
                mha(b, 1)
                norm_turn(b, 7, XR)
                moe(b, 1)

        @block.scalar
        def _(act):
            A = nc.scalar.activation

            act.wait_ge(fold_pe.sem, 1)
            A(AT[:, :], bank[:, 0, 0:P], ACT.Copy).then_inc(fold_ready.sem, 1)
            A(C[:, :], bank[:, 1, 0:P], ACT.Copy).then_inc(fold_ready.sem, 1)

            def norm_save(b, f):
                act.wait_ge(turned.sem, turned.at(b, f + 1))
                A(xT[:, :], bank[:, 7, :], ACT.Copy).then_inc(xT_ready.sem, 1)

            def ffn(b, n):
                for e in range(NE0):
                    o = n * NE0 + e
                    act.wait_ge(z_ready.sem, z_ready.at(b, o + 1))
                    if e >= 2:
                        act.wait_ge(y_ready.sem, y_ready.at(b, n * (NE0 + 1) + e - 1))
                    A(hT[:, e % 2, :], bank[:, e % 2, :], ACT.Relu, bias=b1[:, e:e + 1]).then_inc(h_ready.sem, 1)
                act.wait_ge(routeT_turned.sem, routeT_turned.at(b, n + 1))
                A(wrouteT[:, :], bank[0:NE0, 5, :], ACT.Copy).then_inc(routeT_ready.sem, 1)

            def attn0(b):
                act.wait_ge(qkv_ready.sem, qkv_ready.at(b, 1))
                A(qT[:, :], bank[:, 0, :], ACT.Identity, bias=bqk[:, 0:1]).then_inc(qk_saved.sem, 1)
                act.wait_ge(qkv_ready.sem, qkv_ready.at(b, 2))
                A(kT[:, :], bank[:, 1, :], ACT.Identity, bias=bqk[:, 1:2]).then_inc(qk_saved.sem, 1)
                for t in range(T):
                    w = (t + 1) * P
                    act.wait_ge(bias_ready.sem, bias_ready.at(b, t + 1))
                    if t >= 2:
                        act.wait_ge(p_turned.sem, p_turned.at(b, t - 1))
                    A(probs[:, t % 2, 0:w], bank[:, 3 + t % 2, 0:w], ACT.Exp, bias=neg_bias[:, t:t + 1],
                      scale=float(D) ** -0.5, accum_out=row_sum[:, t:t + 1]).then_inc(p_ready.sem, 1)

            def linear(b):
                for k, dst in enumerate((gram, gramC, mix)):
                    act.wait_ge(lin_ready.sem, lin_ready.at(b, k + 1))
                    A(dst[:, :], bank[:, k, 0:P], ACT.Copy).then_inc(lin_saved.sem, 1)

            def mha(b, m):
                act.wait_ge(rope_ready.sem, rope_ready.at(b, 2 * m + 1))
                A(q_part[:, 0, :], rope_a[:, :], ACT.Copy).then_inc(part0_ready.sem, 1)
                act.wait_ge(rope_ready.sem, rope_ready.at(b, 2 * m + 2))
                A(k_part[:, 0, :], rope_ka[:, :], ACT.Copy).then_inc(part0_ready.sem, 1)
                act.wait_ge(rest_ready.sem, rest_ready.at(b, 2 * m + 1))
                A(q_part[:, 1, :], q_rest[:, :], ACT.Copy).then_inc(part1_ready.sem, 1)
                act.wait_ge(rest_ready.sem, rest_ready.at(b, 2 * m + 2))
                A(k_part[:, 1, :], k_rest[:, :], ACT.Copy).then_inc(part1_ready.sem, 1)

                def nmax_save(hg):
                    act.wait_ge(nmax_turned.sem, nmax_turned.at(b, m * KV + hg + 1))
                    bb = bank[:, 7, :].bitcast(BF16)
                    if hg >= 2:
                        act.wait_ge(nmax_stacked.sem, nmax_stacked.at(b, (m * KV + hg - 1) * 16))
                    A(nmaxT[:, hg % 2, :], bb[0:PART * REP, 0:S], ACT.Copy).then_inc(nmaxT_ready.sem, 1)

                def ot_save(hg):
                    act.wait_ge(av_done.sem, av_done.at(b, (m * KV + hg + 1) * TU))
                    if hg >= 2:
                        act.wait_ge(o_turned.sem, o_turned.at(b, m * KV + hg - 1))
                    A(OT[:, hg % 2, :], bank[:, 6, :], ACT.Copy).then_inc(ot_ready.sem, 1)

                for step in range(KV + 1):
                    if step >= 1:
                        for u in range(TU):
                            n = (m * KV + step - 1) * TU + u
                            act.wait_ge(t_ready.sem, t_ready.at(b, n + 1))
                            if (step - 1) * TU + u >= RING:
                                act.wait_ge(av_done.sem, av_done.at(b, n + 1 - RING))
                            A(E[:, n % RING, :], bank[:, 4 + n % 2, :], ACT.Exp, scale=float(HD) ** -0.5)\
                                .then_inc(e_ready.sem, 1)
                    if step >= 1:
                        ot_save(step - 1)
                    if step < KV:
                        nmax_save(step)
                act.wait_ge(a_turned.sem, a_turned.at(b, m + 1))
                A(aT[:, :], bank[:, 7, :], ACT.Copy).then_inc(aT_ready.sem, 1)

            def moe(b, n):
                act.wait_ge(mshift_ready.sem, mshift_ready.at(b, n + 1))
                A(escore[:, :, :], score2[:, :, 0:NE1], ACT.Exp).then_inc(mexp_ready.sem, 1)
                for u in range(NU):
                    o = n * NU + u
                    act.wait_ge(gated_ready.sem, gated_ready.at(b, o + 1))
                    if u >= 2:
                        act.wait_ge(g_ready.sem, g_ready.at(b, o - 1))
                    A(hT[:, u % 2, :], bank[:, 0, :], ACT.Silu).then_inc(silu_ready.sem, 1)

            with act.Fori(0, B) as b:
                norm_save(b, 0)
                ffn(b, 0)
                norm_save(b, 1)
                attn0(b)
                norm_save(b, 2)
                ffn(b, 1)
                norm_save(b, 3)
                mha(b, 0)
                norm_save(b, 4)
                moe(b, 0)
                norm_save(b, 5)
                linear(b)
                norm_save(b, 6)
                mha(b, 1)
                norm_save(b, 7)
                moe(b, 1)

        @block.gpsimd
        def _(pool):
            G = nc.gpsimd

            def own(i, b):
                pool_own.seen += 1
                i.then_inc(pool_own.sem, 1)
                pool.wait_ge(pool_own.sem, pool_own.at(b, pool_own.seen))
                pool.nop(nofuse=True)

            pool.wait_ge(const_ready.sem, 1)

            def layernorm(b, f):
                pool.wait_ge(stats_ready.sem, stats_ready.at(b, f + 1))
                pool.nop(nofuse=True)
                own(G.tensor_scalar(var_eps[:, :], mv[:, :, 1], LN_EPS, None, ALU.add), b)
                return G.tensor_tensor(rstd[:, :], var_eps[:, :], minus_half[:, :], ALU.pow)

            def ln_only(b, f):
                layernorm(b, f).then_inc(rstd_ready.sem, 1)

            def ln_rms(b, f):
                own(layernorm(b, f), b)
                own(G.tensor_tensor(rsq[:, :], rstd[:, :], rstd[:, :], ALU.mult), b)
                own(G.tensor_tensor(rms_in[:, :], rsq[:, :], mv[:, :, 1], ALU.mult), b)
                own(G.tensor_scalar(var_eps[:, :], rms_in[:, :], RMS_EPS, None, ALU.add), b)
                G.tensor_tensor(rms[:, :], var_eps[:, :], minus_half[:, :], ALU.pow).then_inc(rstd_ready.sem, 1)

            def rms_only(b, f):
                pool.wait_ge(stats_ready.sem, stats_ready.at(b, f + 1))
                pool.nop(nofuse=True)
                own(G.tensor_tensor(rsq[:, :], mv[:, :, 0], mv[:, :, 0], ALU.mult), b)
                own(G.tensor_tensor(rms_in[:, :], rsq[:, :], mv[:, :, 1], ALU.add), b)
                own(G.tensor_scalar(var_eps[:, :], rms_in[:, :], RMS_EPS, None, ALU.add), b)
                G.tensor_tensor(rms[:, :], var_eps[:, :], minus_half[:, :], ALU.pow).then_inc(rstd_ready.sem, 1)

            def mha(b, m):
                def parts(hg):
                    s = hg % 2
                    pool.wait_ge(mx_used.sem, mx_used.at(b, (m * KV + hg + 1) * MXU))
                    pool.nop(nofuse=True)
                    if hg >= 2:
                        pool.wait_ge(nmax_turned.sem, nmax_turned.at(b, m * KV + hg - 1))
                        pool.nop(nofuse=True)
                    view = nmax[:, :, :].rearrange("p j t -> p t j")
                    rest = nrest[:, :, :].rearrange("p j t -> p t j")
                    own(G.tensor_copy(nparts[:, s, :, 0, :], view), b)
                    own(G.tensor_tensor(rest, view, nparts[:, s, :, 0, :], ALU.subtract), b)
                    own(G.tensor_copy(nparts[:, s, :, 1, :], rest), b)
                    G.tensor_tensor(nparts[:, s, :, 2, :], rest, nparts[:, s, :, 1, :], ALU.subtract)\
                        .then_inc(nparts_ready.sem, 1)

                def mask(hg, u):
                    n = (m * KV + hg) * TU + u
                    kind = T_UNITS[u][0]
                    pool.wait_ge(e_ready.sem, e_ready.at(b, n + 1))
                    pool.nop(nofuse=True)
                    slot = E[:, n % RING, :]
                    if kind == "first":
                        v, pat = slot[:, 0:P], [[1, P]]
                    elif kind == "third":
                        v, pat = slot.rearrange("p (a q) -> p a q", a=2)[:, :, 0:P], [[0, 2], [1, P]]
                    else:
                        v, pat = slot[:, 0:2 * P].rearrange("p (a q) -> p a q", a=2), [[0, 2], [1, P]]
                    G.affine_select(out=v, in_=v, compare_op=ALU.is_ge, fill=0.0, base=0, pattern=pat,
                                    channel_multiplier=-1).then_inc(e_masked.sem, 1)

                for step in range(KV + 1):
                    if step >= 1:
                        for u in range(TU):
                            mask(step - 1, u)
                    if step < KV:
                        parts(step)

            with pool.Fori(0, B) as b:
                ln_only(b, 0)
                ln_only(b, 1)
                ln_only(b, 2)
                ln_rms(b, 3)
                mha(b, 0)
                rms_only(b, 4)
                ln_only(b, 5)
                ln_rms(b, 6)
                mha(b, 1)
                rms_only(b, 7)
            assert pool_own.seen == pool_own.per_turn, pool_own.seen

        @block.vector
        def _(dve):
            V_ = nc.vector

            def own(i, b):
                dve_own.seen += 1
                i.then_inc(dve_own.sem, 1)
                dve.wait_ge(dve_own.sem, dve_own.at(b, dve_own.seen))

            dve.wait_ge(loaded.sem, 16 * len(loads))
            V_.memset(minus_half[:, :], -0.5)
            V_.memset(X[:, :, :], 0.0).then_inc(x_free.sem, 16)
            V_.memset(Vp[:, :, :, :], 0.0)
            V_.memset(Ks[64:QK, :, :], 1.0).then_inc(cleared.sem, 1)
            dve.wait_ge(cleared.sem, 1)
            V_.memset(Vp[:, :, :, HD:HD + 1], 1.0)
            V_.tensor_copy(identb[:, :], ident[:, :])
            V_.tensor_copy(causalb[:, :], causal[:, :])
            V_.tensor_scalar(mproj[:, :], mproj[:, :], g[:, 0:1], None, ALU.mult)
            V_.tensor_scalar(gate[:, :], gate[:, :], g[:, 1:2], None, ALU.mult)
            V_.tensor_scalar(w13[:, :, :, :], w13[:, :, :, :], g[:, 1:2], None, ALU.mult)\
                .then_inc(const_ready.sem, 1)

            def moments(b, src):
                for t in range(T):
                    i = V_.bn_stats(stats[:, t, :], src[:, t, :])
                own(i, b)
                dve.nop(nofuse=True)
                for t in range(T):
                    i = V_.bn_aggr(mv[:, t, :], stats[:, t, :])
                i.then_inc(stats_ready.sem, 1)

            def ln(b, f, src, with_rms):
                moments(b, src)
                dve.wait_ge(rstd_ready.sem, rstd_ready.at(b, f + 1))
                for t in range(T):
                    i = V_.tensor_scalar(XN[:, t, :], src[:, t, :], mv[:, t, 0:1], rstd[:, t:t + 1],
                                         ALU.subtract, ALU.mult)
                if with_rms:
                    own(i, b)
                    for t in range(T):
                        i = V_.tensor_scalar(XR[:, t, :], XN[:, t, :], rms[:, t:t + 1], None, ALU.mult)
                i.then_inc(normed.sem, 1)

            def rmsnorm(b, f, src):
                moments(b, src)
                dve.wait_ge(rstd_ready.sem, rstd_ready.at(b, f + 1))
                for t in range(T):
                    i = V_.tensor_scalar(XR[:, t, :], src[:, t, :], rms[:, t:t + 1], None, ALU.mult)
                i.then_inc(normed.sem, 1)

            def wide(v, n):
                return v.unsqueeze(2).to_broadcast([P, T, n])

            def top_two(b, n):
                s = score[:, :, 0:n]
                rk = rank[:, :, NE0 - n:]
                for k in range(2):
                    src = s if k == 0 else score2[:, :, 0:n]
                    tb, hb = tie[:, k, :, 0:n], hot[:, k, :, 0:n]
                    own(V_.tensor_reduce(top[:, 2 * k, :], src, AX_X, ALU.max), b)
                    own(V_.tensor_tensor(tb, src, wide(top[:, 2 * k, :], n), ALU.is_equal), b)
                    own(V_.tensor_tensor(tb, tb, rk, ALU.mult), b)
                    own(V_.tensor_reduce(top[:, 2 * k + 1, :], tb, AX_X, ALU.max), b)
                    own(V_.tensor_tensor(hb, tb, wide(top[:, 2 * k + 1, :], n), ALU.is_equal), b)
                    if k == 0:
                        own(V_.scalar_tensor_tensor(out=score2[:, :, 0:n], in0=hb, scalar=TAKEN, in1=s,
                                                    op0=ALU.mult, op1=ALU.add), b)
                own(V_.tensor_tensor(hot[:, 2, :, 0:n], hot[:, 0, :, 0:n], hot[:, 1, :, 0:n], ALU.add), b)

            def ffn(b, n, src):
                dve.wait_ge(gate_ready.sem, gate_ready.at(b, n + 1))
                own(V_.tensor_tensor(score[:, :, :], bank[:, 4, 0:T * NE0].rearrange("p (t e) -> p t e", t=T),
                                     bg[:, :].unsqueeze(1).to_broadcast([P, T, NE0]), ALU.add), b)
                top_two(b, NE0)
                i = V_.scalar_tensor_tensor(out=wroute[:, :, :], in0=hot[:, 2, :, :], scalar=0.5,
                                            in1=score[:, :, :], op0=ALU.mult, op1=ALU.mult)
                i.then_inc(route_ready.sem, 1)
                dve.wait_ge(route_ready.sem, route_ready.at(b, n + 1))
                for e in range(NE0 + 1):
                    o = n * (NE0 + 1) + e
                    dve.wait_ge(y_ready.sem, y_ready.at(b, o + 1))
                    if e == 0 and n == 0:
                        dve.wait_ge(x_free.sem, x_free.at(b, 16))
                    for t in range(T):
                        base = src if e == 0 else X
                        if e:
                            dve.wait_ge(y_used.sem, y_used.at(b, (o - 1) * T + t + 1))
                        y = bank[:, 2 + e % 2, t * P:(t + 1) * P]
                        if e < NE0:
                            i = V_.scalar_tensor_tensor(out=X[:, t, :], in0=y, scalar=wroute[:, t, e:e + 1],
                                                        in1=base[:, t, :], op0=ALU.mult, op1=ALU.add)
                        else:
                            i = V_.tensor_tensor(X[:, t, :], y, base[:, t, :], ALU.add)
                        i.then_inc(y_used.sem, 1)
                dve.wait_ge(y_used.sem, y_used.at(b, (n + 1) * (NE0 + 1) * T))

            def attn0(b):
                dve.wait_ge(qkv_ready.sem, qkv_ready.at(b, 3))
                V_.tensor_tensor(V[:, :, :], bank[:, 2, :].rearrange("p (t d) -> p t d", t=T),
                                 bv[:, :].unsqueeze(1).to_broadcast([P, T, P]), ALU.add).then_inc(v_saved.sem, 1)

                def save_pT(t):
                    dve.wait_ge(p_turned.sem, p_turned.at(b, t + 1))
                    if t >= 2:
                        dve.wait_ge(o_ready.sem, o_ready.at(b, t - 1))
                    w = (t + 1) * P
                    V_.tensor_copy(probsT[:, t % 2, 0:w], bank[:, 5 + t % 2, 0:w]).then_inc(pT_ready.sem, 1)

                for t in range(T):
                    w = (t + 1) * P
                    dve.wait_ge(s_ready.sem, s_ready.at(b, t + 1))
                    own(V_.tensor_reduce(neg_max[:, t:t + 1], bank[:, 3 + t % 2, 0:w], AX_X, ALU.max,
                                         negate=True), b)
                    V_.tensor_scalar(neg_bias[:, t:t + 1], neg_max[:, t:t + 1], float(D) ** -0.5, None,
                                     ALU.mult).then_inc(bias_ready.sem, 1)
                    if t >= 1:
                        save_pT(t - 1)
                save_pT(T - 1)
                own(V_.reciprocal(row_rec[:, :], row_sum[:, :]), b)
                for t in range(T):
                    dve.wait_ge(o_ready.sem, o_ready.at(b, T))
                    i = V_.scalar_tensor_tensor(out=X[:, t, :], in0=bank[:, 7, t * P:(t + 1) * P],
                                                scalar=row_rec[:, t:t + 1], in1=X[:, t, :],
                                                op0=ALU.mult, op1=ALU.add)
                own(i, b)

            def linear(b):
                dve.wait_ge(normed.sem, normed.at(b, 6))
                own(V_.tensor_tensor(X[:, :, :], X[:, :, :], XN[:, :, :], ALU.add), b)
                dve.wait_ge(lin_ready.sem, lin_ready.at(b, 4))
                own(V_.tensor_tensor(X[:, :, :], bank[:, 3, :].rearrange("p (t d) -> p t d", t=T),
                                     X[:, :, :], ALU.add), b)

            def mha(b, m):
                HK = HD * KV
                dve.wait_ge(proj_ready.sem, proj_ready.at(b, 4 * m + 2))
                V_.tensor_tensor(rope_b[:, :], bank[:, 1, :], sinq[:, :], ALU.mult)
                own(V_.tensor_tensor(rope_a[:, :], bank[:, 0, :], cosq[:, :], ALU.mult), b)
                V_.tensor_tensor(rope_a[:, :], rope_a[:, :], rope_b[:, :], ALU.add).then_inc(rope_ready.sem, 1)
                dve.wait_ge(proj_ready.sem, proj_ready.at(b, 4 * m + 3))
                V_.tensor_tensor(rope_kb[:, :], bank[HK:2 * HK, 2, :], cossink[HK:2 * HK, :], ALU.mult)
                own(V_.tensor_tensor(rope_ka[:, :], bank[0:HK, 2, :], cossink[0:HK, :], ALU.mult), b)
                V_.tensor_tensor(rope_ka[:, :], rope_ka[:, :], rope_kb[:, :], ALU.add).then_inc(rope_ready.sem, 1)
                dve.wait_ge(part0_ready.sem, part0_ready.at(b, 2 * m + 1))
                V_.tensor_tensor(q_rest[:, :], rope_a[:, :], q_part[:, 0, :], ALU.subtract)\
                    .then_inc(rest_ready.sem, 1)
                dve.wait_ge(part0_ready.sem, part0_ready.at(b, 2 * m + 2))
                V_.tensor_tensor(k_rest[:, :], rope_ka[:, :], k_part[:, 0, :], ALU.subtract)\
                    .then_inc(rest_ready.sem, 1)
                dve.wait_ge(proj_ready.sem, proj_ready.at(b, 4 * m + 4))
                V_.tensor_copy(Vp[:, :, :, 0:HD],
                               bank[:, 3, 0:T * HK].rearrange("p (t v d) -> p t v d", t=T, v=KV))\
                    .then_inc(vp_ready.sem, 1)
                dve.wait_ge(part1_ready.sem, part1_ready.at(b, 2 * m + 1))
                V_.tensor_tensor(q_part[:, 2, :], q_rest[:, :], q_part[:, 1, :], ALU.subtract)\
                    .then_inc(part2_ready.sem, 1)
                dve.wait_ge(part1_ready.sem, part1_ready.at(b, 2 * m + 2))
                V_.tensor_tensor(k_part[:, 2, :], k_rest[:, :], k_part[:, 1, :], ALU.subtract)\
                    .then_inc(part2_ready.sem, 1)

                def mx_unit(hg, u):
                    n = (m * KV + hg) * MXU + u
                    dve.wait_ge(mx_ready.sem, mx_ready.at(b, n + 1))
                    if u == 0 and hg:
                        dve.wait_ge(nparts_ready.sem, nparts_ready.at(b, m * KV + hg))
                    b0 = 2 * (u % 2)
                    if u < 4:
                        t = 3 if u < 2 else 2
                        j = 2 * (u % 2)
                        src, dst = bank[:, b0:b0 + 2, 0:(t + 1) * P], nmax[:, j:j + 2, t]
                    elif u == 4:
                        src = bank[:, b0:b0 + 2, :].rearrange("p c (j k) -> p (c j) k", j=2)
                        dst = nmax[:, :, 1]
                    else:
                        src = bank[:, b0, :].rearrange("p (j k) -> p j k", j=4)
                        dst = nmax[:, :, 0]
                    V_.tensor_reduce(dst, src, AX_X, ALU.max, negate=True).then_inc(mx_used.sem, 1)

                def normalize(hg):
                    dve.wait_ge(o_turned.sem, o_turned.at(b, m * KV + hg + 1))
                    o = bank[:, 7, :].rearrange("p (t j r) -> p t j r", t=T, j=REP)
                    own(V_.reciprocal(den[:, :, :], o[:, :, :, HD]), b)
                    for t in range(T):
                        i = V_.tensor_tensor(heads_out[:, t, hg * REP:(hg + 1) * REP, :], o[:, t, :, 0:HD],
                                             den[:, t, :].unsqueeze(2).to_broadcast([P, REP, HD]), ALU.mult)
                    i.then_inc(heads_ready.sem, 1)

                for step in range(KV + 1):
                    if step < KV:
                        for u in range(MXU):
                            mx_unit(step, u)
                    if step >= 1:
                        normalize(step - 1)
                dve.wait_ge(attn_ready.sem, attn_ready.at(b, m + 1))
                own(V_.tensor_tensor(Y[:, :, :], bank[:, 6, :].rearrange("p (t d) -> p t d", t=T),
                                     XN[:, :, :], ALU.add), b)

            def moe(b, n):
                own(V_.scalar_tensor_tensor(out=X[:, :, :], in0=Y[:, :, :], scalar=0.5, in1=X[:, :, :],
                                            op0=ALU.mult, op1=ALU.add), b)
                dve.wait_ge(mgate_ready.sem, mgate_ready.at(b, n + 1))
                s = score[:, :, 0:NE1]
                own(V_.tensor_copy(s, bank[:, 4, 0:T * NE1].rearrange("p (t e) -> p t e", t=T)), b)
                top_two(b, NE1)
                V_.tensor_tensor(score2[:, :, 0:NE1], s, wide(top[:, 0, :], NE1), ALU.subtract)\
                    .then_inc(mshift_ready.sem, 1)

                def weights():
                    dve.wait_ge(mexp_ready.sem, mexp_ready.at(b, n + 1))
                    own(V_.tensor_tensor(epick[:, :, :], escore[:, :, :], hot[:, 2, :, 0:NE1], ALU.mult), b)
                    own(V_.tensor_reduce(esum[:, 0, :], epick[:, :, :], AX_X, ALU.add), b)
                    own(V_.reciprocal(esum[:, 1, :], esum[:, 0, :]), b)
                    own(V_.scalar_tensor_tensor(out=wroute[:, :, 0:NE1], in0=epick[:, :, :], scalar=0.5,
                                                in1=wide(esum[:, 1, :], NE1), op0=ALU.mult, op1=ALU.mult), b)

                def gated(u):
                    o = n * NU + u
                    dve.wait_ge(up_ready.sem, up_ready.at(b, o + 1))
                    dve.wait_ge(silu_ready.sem, silu_ready.at(b, o + 1))
                    V_.tensor_tensor(gT[:, u % 2, :], bank[:, 1, :], hT[:, u % 2, :], ALU.mult)\
                        .then_inc(g_ready.sem, 1)

                def combine(e):
                    o = n * NE1 + e
                    dve.wait_ge(down_ready.sem, down_ready.at(b, o + 1))
                    for t in range(T):
                        if e:
                            dve.wait_ge(down_used.sem, down_used.at(b, (o - 1) * T + t + 1))
                        V_.scalar_tensor_tensor(out=X[:, t, :], in0=bank[:, 2 + e % 2, t * P:(t + 1) * P],
                                                scalar=wroute[:, t, e:e + 1], in1=X[:, t, :],
                                                op0=ALU.mult, op1=ALU.add).then_inc(down_used.sem, 1)

                gated(0)
                weights()
                for u in range(1, NU):
                    gated(u)
                    if u % CH == 1 and u > CH:
                        combine(u // CH - 1)
                combine(NE1 - 1)
                dve.wait_ge(down_used.sem, down_used.at(b, (n + 1) * NE1 * T))

            with dve.Fori(0, B) as b:
                dve.wait_ge(x_loaded.sem, x_loaded.at(b, 16))
                ln(b, 0, Xin, False)
                ffn(b, 0, Xin)
                ln(b, 1, X, False)
                attn0(b)
                ln(b, 2, X, False)
                ffn(b, 1, X)
                ln(b, 3, X, True)
                mha(b, 0)
                rmsnorm(b, 4, Y)
                moe(b, 0)
                ln(b, 5, X, False)
                linear(b)
                ln(b, 6, X, True)
                mha(b, 1)
                rmsnorm(b, 7, Y)
                moe(b, 1)
            assert dve_own.seen == dve_own.per_turn, dve_own.seen


def _rope_tables(np, S, dims, heads):
    inv = (1.0 / 10000.0 ** (np.arange(0, dims, 2, dtype=np.float32) / np.float32(dims))).astype(np.float32)
    freqs = np.arange(S, dtype=np.float32)[:, None] * inv[None, :]
    emb = np.concatenate([freqs, freqs], axis=-1).T
    sign = np.where(np.arange(dims) < dims // 2, -1.0, 1.0).astype(np.float32)[:, None]
    return (np.repeat(np.cos(emb).astype(np.float32), heads, axis=0),
            np.repeat(np.sin(emb).astype(np.float32) * sign, heads, axis=0))


def kernel(**inputs):
    import numpy as np
    import concourse.bacc as bacc
    from concourse.bass_utils import run_bass_kernel_spmd

    H, KV, HD = 16, 4, 8
    x = inputs["L0_attn_x"]
    B, S, D = x.shape

    def by_dim(w, heads):
        return w.reshape(D, heads, HD).transpose(0, 2, 1).reshape(D, heads * HD)

    def swapped(w):
        return w.reshape(D, 2, -1)[:, ::-1, :].reshape(D, -1)

    W, b = inputs["L0_attn_W"], inputs["L0_attn_b"]
    wq, wk = by_dim(inputs["L1_ffn_wq"], H), by_dim(inputs["L1_ffn_wk"], KV)
    cosq, sinq = _rope_tables(np, S, HD, H)
    cosk, sink = _rope_tables(np, S, HD, KV)
    arrays = {
        "x": x, "W_gate": inputs["L0_ffn_W_gate"], "b_gate": inputs["L0_ffn_b_gate"],
        "W1": inputs["L0_ffn_W1"], "b1T": inputs["L0_ffn_b1"].T, "W2": inputs["L0_ffn_W2"],
        "b2": inputs["L0_ffn_b2"], "W": W, "bqk": b[0:2 * D].reshape(2, D).T, "bv": b[2 * D:],
        "WqT": inputs["L1_attn_Wq"].T, "WkT": inputs["L1_attn_Wk"].T, "WvT": inputs["L1_attn_Wv"].T,
        "P": inputs["L1_attn_P"], "g1": inputs["L1_ffn_g1"].reshape(D, 1), "g2": inputs["L1_ffn_g2"].reshape(D, 1),
        "wq": wq, "wq_swap": swapped(wq), "wk": wk, "wk_swap": swapped(wk), "wv": inputs["L1_ffn_wv"],
        "wo": inputs["L1_ffn_wo"], "gate": inputs["L1_ffn_gate"], "w1": inputs["L1_ffn_w1"],
        "w2": inputs["L1_ffn_w2"], "w3": inputs["L1_ffn_w3"],
        "ident": np.eye(D, dtype=np.float32),
        "causal": np.triu(np.full((D, D), MASKED, dtype=np.float32), 1),
        "cosq": cosq, "sinq": sinq, "cossink": np.concatenate([cosk, sink], axis=0),
        "rank": np.broadcast_to(np.arange(8, 0, -1, dtype=np.float32), (D, S // D, 8)),
    }
    nc = bacc.Bacc("TRN2", target_bir_lowering=False, num_devices=1)
    feed, ins = {}, {}
    for name, a in arrays.items():
        a = np.ascontiguousarray(a)
        feed[f"in_{name}"] = a
        ins[name] = nc.dram_tensor(f"in_{name}", a.shape, mybir.dt.from_np(a.dtype), kind="ExternalInput").ap()
    out = nc.dram_tensor("out_x", (B, S, D), F32, kind="ExternalOutput").ap()
    macaron_kernel(nc, ins, out)
    r = run_bass_kernel_spmd(nc, [feed], core_ids=[0])
    return r.results[0]["out_x"]
```

```python
from contextlib import ExitStack

import concourse.bass as bass
from concourse import mybir

F32 = mybir.dt.float32
BF16 = mybir.dt.bfloat16
ALU = mybir.AluOpType
ACT = mybir.ActivationFunctionType
AX_X = mybir.AxisListType.X

DVE_OWN, POOL_OWN = 176, 88
P = 128
LN_EPS = 1e-5
RMS_EPS = 1.1920928955078125e-07
MASKED = -1.0e30
TAKEN = -3.0e38


class Nth:

    def __init__(self, turn, step, first):
        self.turn, self.step, self.first = turn, step, first

    def times(self, n, plus=0):
        fixed = self.first * n + plus
        if isinstance(self.turn, int):
            return self.turn * self.step * n + fixed
        return self.turn * (self.step * n) + fixed

    def is_zeroth(self):
        return isinstance(self.turn, int) and self.turn * self.step + self.first == 0


class Rises:

    def __init__(self, sem, each):
        self.sem, self.each = sem, each

    def at(self, nth, n):
        return nth.times(self.each, n)


class Own:

    def __init__(self, sem, per_turn):
        self.sem, self.per_turn = sem, per_turn
        self.count, self.turn = 0, None

    def enter(self, turn, first):
        self.turn, self.first, self.start = turn, first, self.count

    def leave(self, turns):
        assert self.count - self.start == self.per_turn, self.count - self.start
        self.count, self.turn = self.start + turns * self.per_turn, None

    def rise(self, eng, ins):
        self.count += 1
        ins.then_inc(self.sem, 1)
        if self.turn is None:
            eng.wait_ge(self.sem, self.count)
        else:
            eng.wait_ge(self.sem, self.turn * self.per_turn + (self.count - self.first * self.per_turn))


def macaron_kernel(nc, ins, out):
    x_dram = ins["x"]
    B, S, D = x_dram.shape
    T = S // P
    NE0 = ins["W1"].shape[0]
    NE1, _, HID = ins["w1"].shape
    CH = HID // P
    NU = NE1 * CH
    H, KV = 16, 4
    REP = H // KV
    HD = D // H
    HK = HD * KV
    PART = 3
    ROWS = PART * PART * HD
    MAXROW = 96
    assert ROWS <= MAXROW
    TURNS = B // 2
    assert D == P and T == 4 and HD == 8 and REP == 4 and CH == 3 and B % 2 == 0 and TURNS >= 3

    NSTACK = 2 * PART * PART + 1
    MXU, TU, PAIRS = 11, 10, 5
    RING = 6

    RING0, RING_BANKS, AV = (0, 4), 3, (3, 7)
    S0, S1, Y0, Y1 = (0, 4), (1, 5), (2, 6), (3, 7)

    FRONT_W = [3.5, 4.5, 3]
    FFN_W = FRONT_W + [2.5] * NE0 + [2, 2, 1]
    ATTN0_W = FRONT_W + [4] + [3.6] * (T + 2)
    MOE_W = [4, 3] + FRONT_W + [3] + [3.5] * (NU + 2)
    LINEAR_W = FRONT_W + [2] * 4
    FRONT, FFN, ATTN0, MOE, LINEAR = len(FRONT_W), len(FFN_W), len(ATTN0_W), len(MOE_W), len(LINEAR_W)
    PRE_W = FRONT_W + [8, 8, 12]

    def mx_tick(g, u): return MXU * g + u
    def nmax_tick(g): return MXU * g + MXU + 2
    def t_tick(g, u): return MXU * g + MXU + 7 + u
    def av_tick(g, v): return t_tick(g, 2 * v + 1) + 3
    def oturn_tick(g): return av_tick(g, PAIRS - 1) + 2
    HEADS = oturn_tick(KV - 1) + 1

    HEADS_W = [1.3] * HEADS

    WARM = 2

    MX_AT = {mx_tick(g, u): (g, u) for g in range(KV) for u in range(MXU)}
    NMAX_AT = {nmax_tick(g): g for g in range(KV)}
    T_AT = {t_tick(g, u): (g, u) for g in range(KV) for u in range(TU)}
    AV_AT = {av_tick(g, v): (g, v) for g in range(KV) for v in range(PAIRS)}
    OTURN_AT = {oturn_tick(g): g for g in range(KV)}

    RING_USES = []
    for k in range(HEADS):
        RING_USES += [("mx", MX_AT[k])] if k in MX_AT else []
        RING_USES += [("nmax", NMAX_AT[k])] if k in NMAX_AT else []
        RING_USES += [("t", T_AT[k])] if k in T_AT else []

    def ring_bank(use, s):
        return RING0[s] + RING_USES.index(use) % RING_BANKS

    T_UNITS = []
    for a in (0, 2):
        T_UNITS += [("first", a), ("first", a + 1), ("third", a), ("rest", a), ("rest", a + 1)]
    assert len(T_UNITS) == TU

    def pieces(unit):
        kind, a = unit
        if kind == "first":
            return [(0, a, 0, 0)]
        if kind == "third":
            return [(0, a, 2, 2), (2 * P, a + 1, 2, 2)]
        return [(0, a, 3, 3), (P, a, 1, 1)]

    MX_UNITS = [(3, [j]) for j in range(REP)] + [(2, [j]) for j in range(REP)] + [(1, [0, 1]), (1, [2, 3]),
                                                                                (0, [0, 1, 2, 3])]
    assert len(MX_UNITS) == MXU

    with ExitStack() as ctx:
        def sb(name, shape, dt=F32):
            return ctx.enter_context(nc.sbuf_tensor(name, shape, dt))

        def pair(name, shape, dt=F32):
            return [sb(f"{name}_{s}", shape, dt) for s in range(2)]

        def rises(name, each=1):
            return [Rises(ctx.enter_context(nc.semaphore(f"{name}_{s}")), each) for s in range(2)]

        def once(name):
            return Rises(ctx.enter_context(nc.semaphore(name)), 1)

        bank = ctx.enter_context(nc.psum_tensor("bank", [P, 8, 512], F32))

        ident = sb("ident", [P, P])
        identb = sb("identb", [P, P], BF16)
        causal = sb("causal", [P, P])
        causalb = sb("causalb", [P, P], BF16)
        rank = sb("rank", [P, T, NE0])
        minus_half = sb("minus_half", [P, T])
        cosq = sb("cosq", [P, S])
        sinq = sb("sinq", [P, S])
        cossink = sb("cossink", [2 * HK, S])
        Wg = sb("Wg", [P, NE0])
        bg = sb("bg", [P, NE0])
        W1 = sb("W1", [P, NE0, P])
        b1 = sb("b1", [P, NE0])
        W2 = sb("W2", [P, NE0, P])
        b2 = sb("b2", [NE0, P])
        Wqkv = sb("Wqkv", [P, 3 * P])
        bqk = sb("bqk", [P, 2])
        bv = sb("bv", [P, P])
        WqT = sb("WqT", [P, P])
        WkT = sb("WkT", [P, P])
        WvT = sb("WvT", [P, P])
        Wp = sb("Wp", [P, P])
        AT = sb("AT", [P, P])
        C = sb("C", [P, P])
        gain = sb("gain", [P, 2])
        mproj = sb("mproj", [P, 2 * P + 3 * HK])
        wo = sb("wo", [P, P])
        gate = sb("gate", [P, NE1])
        w13 = sb("w13", [P, 2, NE1, HID])
        w2 = sb("w2", [P, NE1, CH, P])
        w_q, w_qs = mproj[:, 0:P], mproj[:, P:2 * P]
        w_kk = mproj[:, 2 * P:2 * P + 2 * HK]
        w_v = mproj[:, 2 * P + 2 * HK:]

        Xin = pair("Xin", [P, T, P])
        X = pair("X", [P, T, P])
        XN = pair("XN", [P, T, P])
        Y = pair("Y", [P, T, P])
        XR = pair("XR", [P, T, P])
        xT = pair("xT", [P, S])
        stats = pair("stats", [P, T, 6])
        mv = pair("mv", [P, T, 2])
        var_eps = pair("var_eps", [P, T])
        rstd = pair("rstd", [P, T])
        rsq = pair("rsq", [P, T])
        rms_in = pair("rms_in", [P, T])
        rms = pair("rms", [P, T])

        score = pair("score", [P, T, NE0])
        score2 = pair("score2", [P, T, NE0])
        top = pair("top", [P, 4, T])
        tie = pair("tie", [P, 2, T, NE0])
        hot = pair("hot", [P, 3, T, NE0])
        escore = pair("escore", [P, T, NE1])
        epick = pair("epick", [P, T, NE1])
        esum = pair("esum", [P, 2, T])
        wroute = pair("wroute", [P, T, NE0])
        wrouteT = pair("wrouteT", [NE0, S])

        GR = 3
        work = pair("work", [P, 9, S])

        def area(first, count, rows=P):
            return [w[0:rows, first:first + count, :] for w in work]

        def single(first, rows=P):
            return [w[0:rows, first, :] for w in work]

        hT = area(0, 2)
        tanhT, h1T, upT, gT = area(0, 2), area(2, 2), area(4, 2), area(6, GR)
        qT, kT, V = single(0), single(1), [w[:, 2, :].rearrange("p (t d) -> p t d", t=T) for w in work]
        probs, probsT = area(3, 2), area(5, 2)
        rope_a, rope_b, q_rest = single(0), single(1), single(2)
        rope_ka, rope_kb, k_rest = single(3, HK), single(4, HK), single(5, HK)
        E, OT = area(0, RING), area(RING, 2)

        neg_max = pair("neg_max", [P, T])
        neg_bias = pair("neg_bias", [P, T])
        row_sum = pair("row_sum", [P, T])
        row_rec = pair("row_rec", [P, T])

        gram = pair("gram", [P, P])
        gramC = pair("gramC", [P, P])
        mix = pair("mix", [P, P])

        q_part = pair("q_part", [P, PART, S], BF16)
        k_part = pair("k_part", [HK, PART, S], BF16)
        Qs = pair("Qs", [P, H, S], BF16)
        Ks = pair("Ks", [P, KV, S], BF16)
        zeros = sb("zeros", [P, 1, S], BF16)
        Vp = pair("Vp", [P, T, KV, 32])
        nmax = pair("nmax", [P, 2, REP, T])
        nrest = pair("nrest", [P, REP, T])
        nparts = pair("nparts", [P, 2, T, PART, REP], BF16)
        nmaxT = pair("nmaxT", [PART * REP, 2, S], BF16)
        den = pair("den", [P, T, REP])
        heads_out = pair("heads_out", [P, T, H, HD])
        aT = pair("aT", [P, S])

        loaded = once("loaded")
        cleared = once("cleared")
        const_ready = once("const_ready")
        fold_pe = once("fold_pe")
        fold_ready = once("fold_ready")
        x_loaded = rises("x_loaded", 16)
        x_free = rises("x_free", 16)
        stats_ready = rises("stats_ready")
        rstd_ready = rises("rstd_ready")
        normed = rises("normed")
        turned = rises("turned")
        xT_ready = rises("xT_ready")
        gate_ready = rises("gate_ready")
        gate_read = rises("gate_read")
        route_ready = rises("route_ready")
        routeT_turned = rises("routeT_turned")
        routeT_ready = rises("routeT_ready")
        z_ready = rises("z_ready", NE0)
        h_ready = rises("h_ready", NE0)
        y_ready = rises("y_ready", NE0 + 1)
        y_used = rises("y_used", NE0 * T)
        mgate_ready = rises("mgate_ready")
        mgate_read = rises("mgate_read")
        mshift_ready = rises("mshift_ready")
        mexp_ready = rises("mexp_ready")
        h1_ready = rises("h1_ready", NU)
        h3_ready = rises("h3_ready", NU)
        tanh_ready = rises("tanh_ready", NU)
        h1_saved = rises("h1_saved", NU)
        up_ready = rises("up_ready", NU)
        g_ready = rises("g_ready", NU)
        down_done = rises("down_done", NU)
        down_used = rises("down_used", NE1 * T)
        qkv_ready = rises("qkv_ready", 3)
        qk_saved = rises("qk_saved", 2)
        v_saved = rises("v_saved")
        s_ready = rises("s_ready", T)
        bias_ready = rises("bias_ready", T)
        p_ready = rises("p_ready", T)
        p_turned = rises("p_turned", T)
        pT_ready = rises("pT_ready", T)
        o_ready = rises("o_ready", T)
        lin_ready = rises("lin_ready", 4)
        lin_saved = rises("lin_saved", 3)
        proj_ready = rises("proj_ready", 4)
        rope_mul = rises("rope_mul", 2)
        rope_ready = rises("rope_ready", 2)
        part0_ready = rises("part0_ready", 2)
        rest_ready = rises("rest_ready", 2)
        part1_ready = rises("part1_ready", 2)
        part2_ready = rises("part2_ready", 2)
        v_ready = rises("v_ready")
        stacked = rises("stacked", NSTACK * 16)
        mx_ready = rises("mx_ready", KV * MXU)
        mx_used = rises("mx_used", KV * MXU)
        nparts_ready = rises("nparts_ready", KV)
        nmax_turned = rises("nmax_turned", KV)
        nmaxT_ready = rises("nmaxT_ready", KV)
        nmax_stacked = rises("nmax_stacked", KV * 16)
        t_ready = rises("t_ready", KV * TU)
        e_ready = rises("e_ready", KV * TU)
        e_masked = rises("e_masked", KV * TU)
        av_done = rises("av_done", KV * PAIRS)
        ot_ready = rises("ot_ready", KV)
        o_turned = rises("o_turned", KV)
        heads_ready = rises("heads_ready", KV)
        a_turned = rises("a_turned")
        aT_ready = rises("aT_ready")
        attn_ready = rises("attn_ready")
        dve_own = Own(ctx.enter_context(nc.semaphore("dve_own")), DVE_OWN)
        pool_own = Own(ctx.enter_context(nc.semaphore("pool_own")), POOL_OWN)

        x_v = x_dram.rearrange("b (t p) d -> b p t d", p=P)
        out_v = out.rearrange("b (t p) d -> b p t d", p=P)

        loads = [
            (Wg[:, :], ins["W_gate"]), (bg[:, :], ins["b_gate"].partition_broadcast(P)), (ident[:, :], ins["ident"]),
            (rank[:, :, :], ins["rank"]), (b1[:, :], ins["b1T"]), (b2[:, :], ins["b2"]),
            (W1[:, :, :], ins["W1"].rearrange("e d h -> d e h")), (W2[:, :, :], ins["W2"].rearrange("e d h -> d e h")),
            (causal[:, :], ins["causal"]), (cosq[:, :], ins["cosq"]),
            (sinq[:, :], ins["sinq"]), (cossink[:, :], ins["cossink"]),
            (Wqkv[:, :], ins["W"]), (bqk[:, :], ins["bqk"]), (bv[:, :], ins["bv"].partition_broadcast(P)),
            (WqT[:, :], ins["WqT"]), (WkT[:, :], ins["WkT"]), (WvT[:, :], ins["WvT"]), (Wp[:, :], ins["P"]),
            (gain[:, 0:1], ins["g1"]), (gain[:, 1:2], ins["g2"]),
            (w_q, ins["wq"]), (w_qs, ins["wq_swap"]), (w_kk[:, 0:HK], ins["wk"]),
            (w_kk[:, HK:], ins["wk_swap"]), (w_v, ins["wv"]), (wo[:, :], ins["wo"]),
            (gate[:, :], ins["gate"]), (w13[:, 0, :, :], ins["w1"].rearrange("e d h -> d e h")),
            (w13[:, 1, :, :], ins["w3"].rearrange("e d h -> d e h")),
            (w2[:, :, :, :], ins["w2"].rearrange("e (c p) d -> p e c d", p=P)),
        ]

        def idle(ticks):
            for _ in range(ticks):
                yield

        def weave(*streams):
            ahead = [[(w, program) for weights, program in stream for w in weights] for stream in streams]
            walked = [0.0 for _ in ahead]
            while any(ahead):
                k = min((k for k, ticks in enumerate(ahead) if ticks), key=lambda k: walked[k] + ahead[k][0][0])
                w, program = ahead[k].pop(0)
                next(program)
                walked[k] += w
            for stream in streams:
                for _, program in stream:
                    assert next(program, "end") == "end"

        def walk(ffn, attn0, linear, moe, pre, heads, eng, own=None):

            def layer0(t, c, s):
                def nth(step, k):
                    return Nth(t + s, step, step * (c - s) + k)
                return [(FFN_W, ffn(nth(2, 0), nth(8, 0), s, nth(1, 0))),
                        (ATTN0_W, attn0(nth(1, 0), nth(8, 1), s)),
                        (FFN_W, ffn(nth(2, 1), nth(8, 2), s, None)),
                        (PRE_W, pre(nth(2, 0), nth(8, 3), s))]

            def rest(t, s, last):
                def nth(step, k):
                    return Nth(t + s, step, k - step * s)
                return [(HEADS_W, heads(nth(2, 0), s)),
                        (MOE_W, moe(nth(2, 0), nth(8, 4), s, None, None if last else nth(1, 1))),
                        (LINEAR_W, linear(nth(1, 0), nth(8, 5), s)),
                        (PRE_W, pre(nth(2, 1), nth(8, 6), s)), (HEADS_W, heads(nth(2, 1), s)),
                        (MOE_W, moe(nth(2, 1), nth(8, 7), s, nth(1, 0), None))]

            def turn(t, last):
                weave(layer0(t, 0, 0) + rest(t, 0, last), rest(t, 1, last) + ([] if last else layer0(t, 1, 1)))

            weave(layer0(0, 0, 1))
            turn(0, False)
            with eng.Fori(1, TURNS - 1) as t:
                if own:
                    own.enter(t, 1)
                turn(t, False)
            if own:
                own.leave(TURNS - 2)
            turn(TURNS - 1, True)

        block = ctx.enter_context(nc.Block())

        @block.sync
        def _(sp):
            for stream in (1, 0):
                sp.dma_start(Xin[stream][:, :, :], x_v[stream]).then_inc(x_loaded[stream].sem, 16)
            for dst, src in loads:
                sp.dma_start(dst, src).then_inc(loaded.sem, 16)

            def ffn(n, f, s, batch):
                yield from idle(FFN)

            def attn0(n, f, s):
                yield from idle(ATTN0)

            def linear(n, f, s):
                yield from idle(LINEAR)

            def moe(n, f, s, batch, load):
                if load is not None:
                    sp.wait_ge(y_used[s].sem, y_used[s].at(n, T))
                    sp.dma_start(Xin[s][:, :, :], x_v[load.times(2, s)]).then_inc(x_loaded[s].sem, 16)
                yield from idle(MOE - 1)
                if batch is not None:
                    sp.wait_ge(down_used[s].sem, down_used[s].at(n, NE1 * T))
                    sp.dma_start(out_v[batch.times(2, s)], X[s][:, :, :]).then_inc(x_free[s].sem, 16)
                yield

            def pre(n, f, s):
                yield from idle(FRONT + 1)
                for a, ready in enumerate((part0_ready, part1_ready, part2_ready)):
                    sp.wait_ge(ready[s].sem, ready[s].at(n, 1))
                    for c in range(PART):
                        r = (c * PART + a) * HD
                        sp.dma_start(Ks[s][r:r + HD, :, :], k_part[s][:, a, :]).then_inc(stacked[s].sem, 16)
                    sp.wait_ge(ready[s].sem, ready[s].at(n, 2))
                    for c in range(PART):
                        r = (a * PART + c) * HD
                        sp.dma_start(Qs[s][r:r + HD, :, :], q_part[s][:, a, :]).then_inc(stacked[s].sem, 16)
                    if a == 0:
                        sp.dma_start(Qs[s][MAXROW:MAXROW + PART, :, :],
                                     zeros[0:PART, :, :].to_broadcast([PART, H, S])).then_inc(stacked[s].sem, 16)
                    if a != 1:
                        yield

            def heads(n, s):
                for k in range(HEADS):
                    if k in NMAX_AT:
                        g = NMAX_AT[k]
                        sp.wait_ge(nmaxT_ready[s].sem, nmaxT_ready[s].at(n, g + 1))
                        sp.dma_start(Qs[s][MAXROW:MAXROW + PART, g * REP:(g + 1) * REP, :],
                                     nmaxT[s][:, g % 2, :]).then_inc(nmax_stacked[s].sem, 16)
                    yield

            walk(ffn, attn0, linear, moe, pre, heads, sp)
            for stream in range(2):
                sp.wait_ge(x_free[stream].sem, 16 * TURNS)

        @block.tensor
        def _(pe):
            mm = nc.tensor.matmul

            def tr4(dst_bank, src, signal):
                for t in range(T):
                    i = nc.tensor.transpose(bank[:, dst_bank, t * P:(t + 1) * P], src[:, t, :], ident[:, :])
                i.then_inc(signal.sem, 1)

            pe.wait_ge(loaded.sem, 16 * len(loads))
            pe.wait_ge(const_ready.sem, 1)
            mm(bank[:, 0, 0:P], WkT[:, :], WqT[:, :], start=True, stop=True)
            mm(bank[:, 1, 0:P], WvT[:, :], Wp[:, :], start=True, stop=True).then_inc(fold_pe.sem, 1)
            pe.wait_ge(fold_ready.sem, 2)

            def keep_warm(b, count):
                for _ in range(count):
                    mm(bank[:, b, :], identb[:, :], zeros[:, 0, :], start=True, stop=True)

            def front(f, s, src, idle_bank):
                keep_warm(idle_bank, WARM)
                yield
                keep_warm(idle_bank, WARM)
                yield
                keep_warm(idle_bank, WARM)
                pe.wait_ge(normed[s].sem, normed[s].at(f, 1))
                tr4(Y0[s], src, turned[s])
                yield

            def ffn(n, f, s, batch):
                yield from front(f, s, XN[s], S0[s])
                x = xT[s][:, :]
                for e in range(NE0 + 1):
                    if e == 0:
                        pe.wait_ge(xT_ready[s].sem, xT_ready[s].at(f, 1))
                        for t in range(T):
                            i = mm(bank[:, Y0[s], t * NE0:(t + 1) * NE0], x[:, t * P:(t + 1) * P], Wg[:, :],
                                   start=True, stop=True)
                        i.then_inc(gate_ready[s].sem, 1)
                    if e < NE0:
                        if e >= 2:
                            pe.wait_ge(h_ready[s].sem, h_ready[s].at(n, e - 1))
                        mm(bank[:, S0[s] + e % 2, :], W1[:, e, :], x, start=True, stop=True).then_inc(z_ready[s].sem, 1)
                    if e >= 1:
                        d = e - 1
                        pe.wait_ge(h_ready[s].sem, h_ready[s].at(n, d + 1))
                        if d == 1:
                            pe.wait_ge(gate_read[s].sem, gate_read[s].at(n, 1))
                        if d >= 2:
                            pe.wait_ge(y_used[s].sem, y_used[s].at(n, (d - 1) * T))
                        for t in range(T):
                            i = mm(bank[:, (Y1, Y0)[d % 2][s], t * P:(t + 1) * P], hT[s][:, d % 2, t * P:(t + 1) * P], W2[:, d, :],
                                   start=True, stop=True)
                        i.then_inc(y_ready[s].sem, 1)
                    yield
                pe.wait_ge(route_ready[s].sem, route_ready[s].at(n, 1))
                for t in range(T):
                    i = nc.tensor.transpose(bank[0:NE0, S0[s], t * P:(t + 1) * P], wroute[s][:, t, :], ident[:, :])
                i.then_inc(routeT_turned[s].sem, 1)
                yield
                pe.wait_ge(routeT_ready[s].sem, routeT_ready[s].at(n, 1))
                for t in range(T):
                    i = mm(bank[:, S1[s], t * P:(t + 1) * P], wrouteT[s][:, t * P:(t + 1) * P], b2[:, :],
                           start=True, stop=True)
                i.then_inc(y_ready[s].sem, 1)
                yield

            def attn0(n, f, s):
                yield from front(f, s, XN[s], S0[s])
                x = xT[s][:, :]
                pe.wait_ge(xT_ready[s].sem, xT_ready[s].at(f, 1))
                mm(bank[:, S0[s], :], Wqkv[:, 0:P], x, start=True, stop=True).then_inc(qkv_ready[s].sem, 1)
                mm(bank[:, S1[s], :], Wqkv[:, P:2 * P], x, start=True, stop=True).then_inc(qkv_ready[s].sem, 1)
                for t in range(T):
                    i = mm(bank[:, Y0[s], t * P:(t + 1) * P], x[:, t * P:(t + 1) * P], Wqkv[:, 2 * P:],
                           start=True, stop=True)
                i.then_inc(qkv_ready[s].sem, 1)
                yield
                for k in range(T + 2):
                    if k < T:
                        t, w = k, (k + 1) * P
                        if t == 0:
                            pe.wait_ge(qk_saved[s].sem, qk_saved[s].at(n, 2))
                        if t >= 2:
                            pe.wait_ge(p_ready[s].sem, p_ready[s].at(n, t - 1))
                        mm(bank[:, (S0, Y1)[t % 2][s], 0:w], qT[s][:, t * P:(t + 1) * P], kT[s][:, 0:w], start=True, stop=True)
                        mm(bank[:, (S0, Y1)[t % 2][s], t * P:w], identb[:, :], causalb[:, :], start=False, stop=True,
                           skip_group_check=True).then_inc(s_ready[s].sem, 1)
                    if 1 <= k <= T:
                        t = k - 1
                        pe.wait_ge(p_ready[s].sem, p_ready[s].at(n, t + 1))
                        if t:
                            pe.wait_ge(pT_ready[s].sem, pT_ready[s].at(n, t))
                        for j in range(t + 1):
                            i = nc.tensor.transpose(bank[:, S1[s], j * P:(j + 1) * P],
                                                    probs[s][:, t % 2, j * P:(j + 1) * P], ident[:, :])
                        i.then_inc(p_turned[s].sem, 1)
                    if k >= 2:
                        t = k - 2
                        pe.wait_ge(pT_ready[s].sem, pT_ready[s].at(n, t + 1))
                        pe.wait_ge(v_saved[s].sem, v_saved[s].at(n, 1))
                        for j in range(t + 1):
                            i = mm(bank[:, Y0[s], t * P:(t + 1) * P], probsT[s][:, t % 2, j * P:(j + 1) * P], V[s][:, j, :],
                                   start=(t == 0 and j == 0), stop=(j == t), skip_group_check=True)
                        i.then_inc(o_ready[s].sem, 1)
                    yield

            def linear(n, f, s):
                yield from front(f, s, XN[s], S0[s])
                for t in range(T):
                    i = mm(bank[:, S0[s], 0:P], XN[s][:, t, :], XN[s][:, t, :], start=(t == 0), stop=(t == T - 1))
                i.then_inc(lin_ready[s].sem, 1)
                yield
                pe.wait_ge(lin_saved[s].sem, lin_saved[s].at(n, 1))
                mm(bank[:, S1[s], 0:P], gram[s][:, :], C[:, :], start=True, stop=True).then_inc(lin_ready[s].sem, 1)
                yield
                pe.wait_ge(lin_saved[s].sem, lin_saved[s].at(n, 2))
                mm(bank[:, S0[s], 0:P], AT[:, :], gramC[s][:, :], start=True, stop=True).then_inc(lin_ready[s].sem, 1)
                yield
                pe.wait_ge(lin_saved[s].sem, lin_saved[s].at(n, 3))
                pe.wait_ge(xT_ready[s].sem, xT_ready[s].at(f, 1))
                for t in range(T):
                    i = mm(bank[:, Y0[s], t * P:(t + 1) * P], xT[s][:, t * P:(t + 1) * P], mix[s][:, :],
                           start=True, stop=True)
                i.then_inc(lin_ready[s].sem, 1)
                yield

            def moe(n, f, s, batch, load):
                pe.wait_ge(heads_ready[s].sem, heads_ready[s].at(n, KV))
                tr4(Y0[s], heads_out[s][:, :, :, :].rearrange("p t h d -> p t (h d)"), a_turned[s])
                yield
                pe.wait_ge(aT_ready[s].sem, aT_ready[s].at(n, 1))
                for t in range(T):
                    i = mm(bank[:, S0[s], t * P:(t + 1) * P], aT[s][:, t * P:(t + 1) * P], wo[:, :],
                           start=True, stop=True)
                i.then_inc(attn_ready[s].sem, 1)
                keep_warm(S1[s], WARM)
                yield
                yield from front(f, s, XR[s], S1[s])
                x = xT[s][:, :]
                pe.wait_ge(xT_ready[s].sem, xT_ready[s].at(f, 1))
                for t in range(T):
                    i = mm(bank[:, Y0[s], t * NE1:(t + 1) * NE1], x[:, t * P:(t + 1) * P], gate[:, :],
                           start=True, stop=True)
                i.then_inc(mgate_ready[s].sem, 1)
                yield
                for k in range(NU + 2):
                    if k < NU:
                        e, c = divmod(k, CH)
                        if k:
                            pe.wait_ge(h1_saved[s].sem, h1_saved[s].at(n, k))
                        mm(bank[:, S0[s], :], w13[:, 0, e, c * P:(c + 1) * P], x, start=True, stop=True)\
                            .then_inc(h1_ready[s].sem, 1)
                    if k < NU:
                        e, c = divmod(k, CH)
                        if k:
                            pe.wait_ge(up_ready[s].sem, up_ready[s].at(n, k))
                        mm(bank[:, S1[s], :], w13[:, 1, e, c * P:(c + 1) * P], x, start=True, stop=True)\
                            .then_inc(h3_ready[s].sem, 1)
                    if k >= 2:
                        u = k - 2
                        e, c = divmod(u, CH)
                        pe.wait_ge(g_ready[s].sem, g_ready[s].at(n, u + 1))
                        if c == 0 and e == 1:
                            pe.wait_ge(mgate_read[s].sem, mgate_read[s].at(n, 1))
                        if c == 0 and e >= 2:
                            pe.wait_ge(down_used[s].sem, down_used[s].at(n, (e - 1) * T))
                        for t in range(T):
                            i = mm(bank[:, (Y1, Y0)[e % 2][s], t * P:(t + 1) * P], gT[s][:, u % GR, t * P:(t + 1) * P],
                                   w2[:, e, c, :], start=(c == 0 and t == 0), stop=(c == CH - 1),
                                   skip_group_check=True)
                        i.then_inc(down_done[s].sem, 1)
                    yield

            def pre(n, f, s):
                yield from front(f, s, XR[s], S0[s])
                x = xT[s][:, :]
                pe.wait_ge(xT_ready[s].sem, xT_ready[s].at(f, 1))
                mm(bank[0:2 * HK, Y0[s], :], w_kk, x, start=True, stop=True).then_inc(proj_ready[s].sem, 1)
                mm(bank[:, S1[s], :], w_qs, x, start=True, stop=True).then_inc(proj_ready[s].sem, 1)
                mm(bank[:, S0[s], :], w_q, x, start=True, stop=True).then_inc(proj_ready[s].sem, 1)
                yield
                yield
                for t in range(T):
                    i = mm(bank[:, Y1[s], t * HK:(t + 1) * HK], x[:, t * P:(t + 1) * P], w_v, start=True, stop=True)
                i.then_inc(proj_ready[s].sem, 1)
                yield

            def heads(n, s):

                def mx_unit(g, u):
                    t, heads = MX_UNITS[u]
                    b = take_ring(("mx", (g, u)))
                    w = (t + 1) * P
                    for c, j in enumerate(heads):
                        mm(bank[:, b, c * w:(c + 1) * w], Qs[s][:, g * REP + j, t * P:w], Ks[s][:, g, 0:w],
                           start=True, stop=True)
                        i = mm(bank[:, b, c * w + t * P:(c + 1) * w], identb[:, :], causalb[:, :],
                               start=False, stop=True, skip_group_check=True)
                    i.then_inc(mx_ready[s].sem, 1)

                def take_ring(use):
                    r = RING_USES.index(use)
                    if r >= RING_BANKS:
                        what, which = RING_USES[r - RING_BANKS]
                        if what == "mx":
                            g, u = which
                            pe.wait_ge(mx_used[s].sem, mx_used[s].at(n, g * MXU + u + 1))
                        elif what == "t":
                            g, u = which
                            pe.wait_ge(e_ready[s].sem, e_ready[s].at(n, g * TU + u + 1))
                        else:
                            pe.wait_ge(nmaxT_ready[s].sem, nmaxT_ready[s].at(n, which + 1))
                    return ring_bank(use, s)

                def nmax_turn(g):
                    pe.wait_ge(nparts_ready[s].sem, nparts_ready[s].at(n, g + 1))
                    rows = bank[:, take_ring(("nmax", g)), :].bitcast(BF16)
                    for t in range(T):
                        i = nc.tensor.transpose(rows[0:PART * REP, t * P:(t + 1) * P],
                                                nparts[s][:, g % 2, t, :, :].rearrange("p a j -> p (a j)"),
                                                identb[:, :])
                    i.then_inc(nmax_turned[s].sem, 1)

                def t_unit(g, u):
                    if u == 0:
                        pe.wait_ge(nmax_stacked[s].sem, nmax_stacked[s].at(n, (g + 1) * 16))
                    b = take_ring(("t", (g, u)))
                    for col, j, kt, q0 in pieces(T_UNITS[u]):
                        i = mm(bank[:, b, col:col + (T - q0) * P], Ks[s][:, g, kt * P:(kt + 1) * P],
                               Qs[s][:, g * REP + j, q0 * P:], start=True, stop=True)
                    i.then_inc(t_ready[s].sem, 1)

                def av_pair(g, v):
                    pe.wait_ge(e_masked[s].sem, e_masked[s].at(n, g * TU + 2 * v + 2))
                    if v == 0 and g:
                        pe.wait_ge(heads_ready[s].sem, heads_ready[s].at(n, g))
                    both = [(2 * v + c, p) for c in range(2) for p in pieces(T_UNITS[2 * v + c])]
                    for u, (col, j, kt, q0) in both:
                        i = mm(bank[32 * j:32 * j + 32, AV[s], q0 * P:], Vp[s][:, kt, g, :],
                               E[s][:, (g * TU + u) % RING, col:col + (T - q0) * P],
                               start=(kt == 0), stop=True, skip_group_check=True)
                    i.then_inc(av_done[s].sem, 1)

                for k in range(HEADS):
                    if k == 0:
                        pe.wait_ge(stacked[s].sem, stacked[s].at(n, NSTACK * 16))
                        pe.wait_ge(v_ready[s].sem, v_ready[s].at(n, 1))
                    if k in MX_AT:
                        mx_unit(*MX_AT[k])
                    if k in NMAX_AT:
                        nmax_turn(NMAX_AT[k])
                    if k in OTURN_AT:
                        g = OTURN_AT[k]
                        pe.wait_ge(ot_ready[s].sem, ot_ready[s].at(n, g + 1))
                        tr4(AV[s], OT[s][:, g % 2, :].rearrange("p (t q) -> p t q", t=T), o_turned[s])
                    if k in T_AT:
                        t_unit(*T_AT[k])
                    if k in AV_AT:
                        av_pair(*AV_AT[k])
                    yield

            walk(ffn, attn0, linear, moe, pre, heads, pe)

        @block.scalar
        def _(act):
            A = nc.scalar.activation

            act.wait_ge(fold_pe.sem, 1)
            A(AT[:, :], bank[:, 0, 0:P], ACT.Copy).then_inc(fold_ready.sem, 1)
            A(C[:, :], bank[:, 1, 0:P], ACT.Copy).then_inc(fold_ready.sem, 1)

            def front(f, s):
                yield
                yield
                act.wait_ge(turned[s].sem, turned[s].at(f, 1))
                A(xT[s][:, :], bank[:, Y0[s], :], ACT.Copy).then_inc(xT_ready[s].sem, 1)
                yield

            def ffn(n, f, s, batch):
                yield from front(f, s)
                for e in range(NE0):
                    act.wait_ge(z_ready[s].sem, z_ready[s].at(n, e + 1))
                    if e >= 2:
                        act.wait_ge(y_ready[s].sem, y_ready[s].at(n, e - 1))
                    A(hT[s][:, e % 2, :], bank[:, S0[s] + e % 2, :], ACT.Relu, bias=b1[:, e:e + 1])\
                        .then_inc(h_ready[s].sem, 1)
                    yield
                yield
                act.wait_ge(routeT_turned[s].sem, routeT_turned[s].at(n, 1))
                A(wrouteT[s][:, :], bank[0:NE0, S0[s], :], ACT.Copy).then_inc(routeT_ready[s].sem, 1)
                yield
                yield

            def attn0(n, f, s):
                yield from front(f, s)
                act.wait_ge(qkv_ready[s].sem, qkv_ready[s].at(n, 1))
                A(qT[s][:, :], bank[:, S0[s], :], ACT.Identity, bias=bqk[:, 0:1]).then_inc(qk_saved[s].sem, 1)
                act.wait_ge(qkv_ready[s].sem, qkv_ready[s].at(n, 2))
                A(kT[s][:, :], bank[:, S1[s], :], ACT.Identity, bias=bqk[:, 1:2]).then_inc(qk_saved[s].sem, 1)
                yield
                for t in range(T):
                    w = (t + 1) * P
                    act.wait_ge(bias_ready[s].sem, bias_ready[s].at(n, t + 1))
                    if t >= 2:
                        act.wait_ge(p_turned[s].sem, p_turned[s].at(n, t - 1))
                    A(probs[s][:, t % 2, 0:w], bank[:, (S0, Y1)[t % 2][s], 0:w], ACT.Exp, bias=neg_bias[s][:, t:t + 1],
                      scale=float(D) ** -0.5, accum_out=row_sum[s][:, t:t + 1]).then_inc(p_ready[s].sem, 1)
                    yield
                yield
                yield

            def linear(n, f, s):
                yield from front(f, s)
                for k, (dst, b) in enumerate(((gram, S0), (gramC, S1), (mix, S0))):
                    act.wait_ge(lin_ready[s].sem, lin_ready[s].at(n, k + 1))
                    A(dst[s][:, :], bank[:, b[s], 0:P], ACT.Copy).then_inc(lin_saved[s].sem, 1)
                    yield
                yield

            def moe(n, f, s, batch, load):
                act.wait_ge(a_turned[s].sem, a_turned[s].at(n, 1))
                A(aT[s][:, :], bank[:, Y0[s], :], ACT.Copy).then_inc(aT_ready[s].sem, 1)
                yield
                yield
                yield from front(f, s)
                yield
                for u in range(NU):
                    if u == 2:
                        act.wait_ge(mshift_ready[s].sem, mshift_ready[s].at(n, 1))
                        A(escore[s][:, :, :], score2[s][:, :, 0:NE1], ACT.Exp).then_inc(mexp_ready[s].sem, 1)
                    act.wait_ge(h1_ready[s].sem, h1_ready[s].at(n, u + 1))
                    if u >= 2:
                        act.wait_ge(up_ready[s].sem, up_ready[s].at(n, u - 1))
                    A(tanhT[s][:, u % 2, :], bank[:, S0[s], :], ACT.Tanh, scale=0.5).then_inc(tanh_ready[s].sem, 1)
                    if u >= 2:
                        act.wait_ge(g_ready[s].sem, g_ready[s].at(n, u - 1))
                    A(h1T[s][:, u % 2, :], bank[:, S0[s], :], ACT.Copy).then_inc(h1_saved[s].sem, 1)
                    yield
                yield
                yield

            def pre(n, f, s):
                yield from front(f, s)
                act.wait_ge(rope_ready[s].sem, rope_ready[s].at(n, 1))
                A(k_part[s][:, 0, :], rope_ka[s][:, :], ACT.Copy).then_inc(part0_ready[s].sem, 1)
                act.wait_ge(rope_ready[s].sem, rope_ready[s].at(n, 2))
                A(q_part[s][:, 0, :], rope_a[s][:, :], ACT.Copy).then_inc(part0_ready[s].sem, 1)
                yield
                act.wait_ge(rest_ready[s].sem, rest_ready[s].at(n, 1))
                A(k_part[s][:, 1, :], k_rest[s][:, :], ACT.Copy).then_inc(part1_ready[s].sem, 1)
                act.wait_ge(rest_ready[s].sem, rest_ready[s].at(n, 2))
                A(q_part[s][:, 1, :], q_rest[s][:, :], ACT.Copy).then_inc(part1_ready[s].sem, 1)
                yield
                yield

            def heads(n, s):
                for k in range(HEADS):
                    if k in NMAX_AT:
                        g = NMAX_AT[k]
                        act.wait_ge(nmax_turned[s].sem, nmax_turned[s].at(n, g + 1))
                        if g >= 2:
                            act.wait_ge(nmax_stacked[s].sem, nmax_stacked[s].at(n, (g - 1) * 16))
                        rows = bank[:, ring_bank(("nmax", g), s), :].bitcast(BF16)
                        A(nmaxT[s][:, g % 2, :], rows[0:PART * REP, 0:S], ACT.Copy).then_inc(nmaxT_ready[s].sem, 1)
                    if k in T_AT:
                        g, u = T_AT[k]
                        m = g * TU + u
                        act.wait_ge(t_ready[s].sem, t_ready[s].at(n, m + 1))
                        if m >= RING:
                            act.wait_ge(av_done[s].sem, av_done[s].at(n, (m - RING) // 2 + 1))
                        A(E[s][:, m % RING, :], bank[:, ring_bank(("t", (g, u)), s), :], ACT.Exp,
                          scale=float(HD) ** -0.5).then_inc(e_ready[s].sem, 1)
                    if k in AV_AT and AV_AT[k][1] == PAIRS - 1:
                        g = AV_AT[k][0]
                        act.wait_ge(av_done[s].sem, av_done[s].at(n, (g + 1) * PAIRS))
                        if g >= 2:
                            act.wait_ge(o_turned[s].sem, o_turned[s].at(n, g - 1))
                        A(OT[s][:, g % 2, :], bank[:, AV[s], :], ACT.Copy).then_inc(ot_ready[s].sem, 1)
                    yield

            walk(ffn, attn0, linear, moe, pre, heads, act)

        @block.gpsimd
        def _(pool):
            G = nc.gpsimd

            def own(i):
                pool_own.rise(pool, i)
                pool.nop(nofuse=True)

            def wait(signal, nth, n):
                pool.wait_ge(signal.sem, signal.at(nth, n))
                pool.nop(nofuse=True)

            wait(const_ready, Nth(0, 0, 0), 1)

            def front(f, s, layer, root):
                ve, rs, mean, var = var_eps[s][:, :], rstd[s][:, :], mv[s][:, :, 0], mv[s][:, :, 1]
                wait(stats_ready[s], f, 1)
                if layer:
                    own(G.tensor_scalar(ve, var, LN_EPS, None, ALU.add))
                    last = G.tensor_tensor(rs, ve, minus_half[:, :], ALU.pow)
                if root:
                    if layer:
                        own(last)
                        own(G.tensor_tensor(rsq[s][:, :], rs, rs, ALU.mult))
                        own(G.tensor_tensor(rms_in[s][:, :], rsq[s][:, :], var, ALU.mult))
                    else:
                        own(G.tensor_tensor(rsq[s][:, :], mean, mean, ALU.mult))
                        own(G.tensor_tensor(rms_in[s][:, :], rsq[s][:, :], var, ALU.add))
                    own(G.tensor_scalar(ve, rms_in[s][:, :], RMS_EPS, None, ALU.add))
                    last = G.tensor_tensor(rms[s][:, :], ve, minus_half[:, :], ALU.pow)
                last.then_inc(rstd_ready[s].sem, 1)
                yield
                yield
                yield

            def ffn(n, f, s, batch):
                yield from front(f, s, True, False)
                yield from idle(FFN - FRONT)

            def attn0(n, f, s):
                yield from front(f, s, True, False)
                yield from idle(ATTN0 - FRONT)

            def linear(n, f, s):
                yield from front(f, s, True, False)
                yield from idle(LINEAR - FRONT)

            def moe(n, f, s, batch, load):
                yield
                yield
                yield from front(f, s, False, True)
                yield
                for u in range(NU):
                    wait(h1_saved[s], n, u + 1)
                    wait(up_ready[s], n, u + 1)
                    if u >= GR:
                        wait(down_done[s], n, u - GR + 1)
                    G.tensor_tensor(gT[s][:, u % GR, :], upT[s][:, u % 2, :], h1T[s][:, u % 2, :], ALU.mult)\
                        .then_inc(g_ready[s].sem, 1)
                    yield
                yield
                yield

            def pre(n, f, s):
                yield from front(f, s, True, True)
                yield from idle(3)

            def heads(n, s):

                def parts(g):
                    p = nparts[s][:, g % 2]
                    wait(mx_used[s], n, (g + 1) * MXU)
                    if g >= 2:
                        wait(nmax_turned[s], n, g - 1)
                    view = nmax[s][:, g % 2, :, :].rearrange("p j t -> p t j")
                    rest = nrest[s][:, :, :].rearrange("p j t -> p t j")
                    own(G.tensor_copy(p[:, :, 0, :], view))
                    own(G.tensor_tensor(rest, view, p[:, :, 0, :], ALU.subtract))
                    own(G.tensor_copy(p[:, :, 1, :], rest))
                    G.tensor_tensor(p[:, :, 2, :], rest, p[:, :, 1, :], ALU.subtract).then_inc(nparts_ready[s].sem, 1)

                def mask(g, u):
                    wait(e_ready[s], n, g * TU + u + 1)
                    slot = E[s][:, (g * TU + u) % RING, :]
                    kind = T_UNITS[u][0]
                    if kind == "first":
                        v, pat = slot[:, 0:P], [[1, P]]
                    elif kind == "third":
                        v, pat = slot.rearrange("p (a q) -> p a q", a=2)[:, :, 0:P], [[0, 2], [1, P]]
                    else:
                        v, pat = slot[:, 0:2 * P].rearrange("p (a q) -> p a q", a=2), [[0, 2], [1, P]]
                    G.affine_select(out=v, in_=v, compare_op=ALU.is_ge, fill=0.0, base=0, pattern=pat,
                                    channel_multiplier=-1).then_inc(e_masked[s].sem, 1)

                for k in range(HEADS):
                    if k in T_AT:
                        mask(*T_AT[k])
                    if k in MX_AT and MX_AT[k][1] == MXU - 1:
                        parts(MX_AT[k][0])
                    yield

            walk(ffn, attn0, linear, moe, pre, heads, pool, pool_own)

        @block.vector
        def _(dve):
            V_ = nc.vector

            def own(i):
                dve_own.rise(dve, i)

            def tiles(v):
                return v.rearrange("p (t d) -> p t d", t=T)

            V_.memset(minus_half[:, :], -0.5)
            for stream in range(2):
                V_.memset(Vp[stream][:, :, :, :], 0.0)
                V_.memset(Qs[stream][64:P, :, :], 0.0)
                V_.memset(Ks[stream][64:MAXROW, :, :], 0.0)
                V_.memset(Ks[stream][MAXROW:P, :, :], 1.0)
            V_.memset(zeros[:, :, :], 0.0).then_inc(cleared.sem, 1)
            dve.wait_ge(cleared.sem, 1)
            for stream in range(2):
                V_.memset(Vp[stream][:, :, :, HD:HD + 1], 1.0)
            dve.wait_ge(loaded.sem, 16 * len(loads))
            V_.tensor_copy(identb[:, :], ident[:, :])
            V_.tensor_copy(causalb[:, :], causal[:, :])
            V_.tensor_scalar(mproj[:, :], mproj[:, :], gain[:, 0:1], None, ALU.mult)
            V_.tensor_scalar(gate[:, :], gate[:, :], gain[:, 1:2], None, ALU.mult)
            V_.tensor_scalar(w13[:, :, :, :], w13[:, :, :, :], gain[:, 1:2], None, ALU.mult)\
                .then_inc(const_ready.sem, 1)

            def front(f, s, src, layer, root):
                for t in range(T):
                    i = V_.bn_stats(stats[s][:, t, :], src[:, t, :])
                own(i)
                dve.nop(nofuse=True)
                for t in range(T):
                    i = V_.bn_aggr(mv[s][:, t, :], stats[s][:, t, :])
                i.then_inc(stats_ready[s].sem, 1)
                yield
                dve.wait_ge(rstd_ready[s].sem, rstd_ready[s].at(f, 1))
                if layer:
                    for t in range(T):
                        i = V_.tensor_scalar(XN[s][:, t, :], src[:, t, :], mv[s][:, t, 0:1],
                                             rstd[s][:, t:t + 1], ALU.subtract, ALU.mult)
                    src = XN[s]
                if root:
                    if layer:
                        own(i)
                    for t in range(T):
                        i = V_.tensor_scalar(XR[s][:, t, :], src[:, t, :], rms[s][:, t:t + 1], None, ALU.mult)
                i.then_inc(normed[s].sem, 1)
                yield
                yield

            def wide(v, n):
                return v.unsqueeze(2).to_broadcast([P, T, n])

            def largest(k, n, s):
                sc, rk = score[s][:, :, 0:n], rank[:, :, NE0 - n:]
                src, tb, hb = (sc, score2[s][:, :, 0:n])[k], tie[s][:, k, :, 0:n], hot[s][:, k, :, 0:n]
                if k == 1:
                    own(V_.scalar_tensor_tensor(out=src, in0=hot[s][:, 0, :, 0:n], scalar=TAKEN, in1=sc,
                                                op0=ALU.mult, op1=ALU.add))
                own(V_.tensor_reduce(top[s][:, 2 * k, :], src, AX_X, ALU.max))
                own(V_.tensor_tensor(tb, src, wide(top[s][:, 2 * k, :], n), ALU.is_equal))
                own(V_.tensor_tensor(tb, tb, rk, ALU.mult))
                own(V_.tensor_reduce(top[s][:, 2 * k + 1, :], tb, AX_X, ALU.max))
                own(V_.tensor_tensor(hb, tb, wide(top[s][:, 2 * k + 1, :], n), ALU.is_equal))
                if k == 1:
                    own(V_.tensor_tensor(hot[s][:, 2, :, 0:n], hot[s][:, 0, :, 0:n], hb, ALU.add))

            def ffn(n, f, s, batch):
                src = X[s]
                if batch is not None:
                    src = Xin[s]
                    dve.wait_ge(x_loaded[s].sem, batch.times(16, 16))
                yield from front(f, s, src, True, False)
                dve.wait_ge(gate_ready[s].sem, gate_ready[s].at(n, 1))
                V_.tensor_tensor(score[s][:, :, :], bank[:, Y0[s], 0:T * NE0].rearrange("p (t e) -> p t e", t=T),
                                 bg[:, :].unsqueeze(1).to_broadcast([P, T, NE0]), ALU.add)\
                    .then_inc(gate_read[s].sem, 1)
                dve.wait_ge(gate_read[s].sem, gate_read[s].at(n, 1))
                largest(0, NE0, s)
                yield
                largest(1, NE0, s)
                V_.scalar_tensor_tensor(out=wroute[s][:, :, :], in0=hot[s][:, 2, :, :], scalar=0.5,
                                        in1=score[s][:, :, :], op0=ALU.mult, op1=ALU.mult)\
                    .then_inc(route_ready[s].sem, 1)
                dve.wait_ge(route_ready[s].sem, route_ready[s].at(n, 1))
                if batch is not None and not batch.is_zeroth():
                    dve.wait_ge(x_free[s].sem, batch.times(16))
                yield
                for e in range(NE0):
                    dve.wait_ge(y_ready[s].sem, y_ready[s].at(n, e + 1))
                    base = src if e == 0 else X[s][:, :, :]
                    for t in range(T):
                        if e:
                            dve.wait_ge(y_used[s].sem, y_used[s].at(n, (e - 1) * T + t + 1))
                        V_.scalar_tensor_tensor(out=X[s][:, t, :],
                                                in0=bank[:, (Y1, Y0)[e % 2][s], t * P:(t + 1) * P],
                                                scalar=wroute[s][:, t, e:e + 1], in1=base[:, t, :],
                                                op0=ALU.mult, op1=ALU.add).then_inc(y_used[s].sem, 1)
                    yield
                dve.wait_ge(y_ready[s].sem, y_ready[s].at(n, NE0 + 1))
                dve.wait_ge(y_used[s].sem, y_used[s].at(n, NE0 * T))
                for t in range(T):
                    i = V_.tensor_tensor(X[s][:, t, :], bank[:, S1[s], t * P:(t + 1) * P], X[s][:, t, :], ALU.add)
                own(i)
                yield

            def attn0(n, f, s):
                yield from front(f, s, X[s], True, False)
                dve.wait_ge(qkv_ready[s].sem, qkv_ready[s].at(n, 3))
                V_.tensor_tensor(V[s][:, :, :], tiles(bank[:, Y0[s], :]), bv[:, :].unsqueeze(1).to_broadcast([P, T, P]),
                                 ALU.add).then_inc(v_saved[s].sem, 1)
                yield
                for k in range(T + 1):
                    if k < T:
                        t, w = k, (k + 1) * P
                        dve.wait_ge(s_ready[s].sem, s_ready[s].at(n, t + 1))
                        own(V_.tensor_reduce(neg_max[s][:, t:t + 1], bank[:, (S0, Y1)[t % 2][s], 0:w], AX_X, ALU.max, negate=True))
                        V_.tensor_scalar(neg_bias[s][:, t:t + 1], neg_max[s][:, t:t + 1], float(D) ** -0.5, None,
                                         ALU.mult).then_inc(bias_ready[s].sem, 1)
                    if k >= 1:
                        t, w = k - 1, k * P
                        dve.wait_ge(p_turned[s].sem, p_turned[s].at(n, t + 1))
                        if t >= 2:
                            dve.wait_ge(o_ready[s].sem, o_ready[s].at(n, t - 1))
                        V_.tensor_copy(probsT[s][:, t % 2, 0:w], bank[:, S1[s], 0:w]).then_inc(pT_ready[s].sem, 1)
                    yield
                own(V_.reciprocal(row_rec[s][:, :], row_sum[s][:, :]))
                dve.wait_ge(o_ready[s].sem, o_ready[s].at(n, T))
                for t in range(T):
                    i = V_.scalar_tensor_tensor(out=X[s][:, t, :], in0=bank[:, Y0[s], t * P:(t + 1) * P],
                                                scalar=row_rec[s][:, t:t + 1], in1=X[s][:, t, :],
                                                op0=ALU.mult, op1=ALU.add)
                own(i)
                yield

            def linear(n, f, s):
                yield from front(f, s, X[s], True, False)
                yield
                dve.wait_ge(normed[s].sem, normed[s].at(f, 1))
                own(V_.tensor_tensor(X[s][:, :, :], X[s][:, :, :], XN[s][:, :, :], ALU.add))
                yield
                yield
                dve.wait_ge(lin_ready[s].sem, lin_ready[s].at(n, 4))
                own(V_.tensor_tensor(X[s][:, :, :], tiles(bank[:, Y0[s], :]), X[s][:, :, :], ALU.add))
                yield

            def moe(n, f, s, batch, load):
                yield
                dve.wait_ge(attn_ready[s].sem, attn_ready[s].at(n, 1))
                own(V_.tensor_tensor(Y[s][:, :, :], tiles(bank[:, S0[s], :]), XN[s][:, :, :], ALU.add))
                yield
                yield from front(f, s, Y[s], False, True)
                own(V_.scalar_tensor_tensor(out=X[s][:, :, :], in0=Y[s][:, :, :], scalar=0.5, in1=X[s][:, :, :],
                                            op0=ALU.mult, op1=ALU.add))
                dve.wait_ge(mgate_ready[s].sem, mgate_ready[s].at(n, 1))
                sc = score[s][:, :, 0:NE1]
                V_.tensor_copy(sc, bank[:, Y0[s], 0:T * NE1].rearrange("p (t e) -> p t e", t=T))\
                    .then_inc(mgate_read[s].sem, 1)
                dve.wait_ge(mgate_read[s].sem, mgate_read[s].at(n, 1))
                yield
                for k in range(NU + 2):
                    if k == 3:
                        dve.wait_ge(mexp_ready[s].sem, mexp_ready[s].at(n, 1))
                        own(V_.tensor_tensor(epick[s][:, :, :], escore[s][:, :, :], hot[s][:, 2, :, 0:NE1], ALU.mult))
                        own(V_.tensor_reduce(esum[s][:, 0, :], epick[s][:, :, :], AX_X, ALU.add))
                        own(V_.reciprocal(esum[s][:, 1, :], esum[s][:, 0, :]))
                        own(V_.scalar_tensor_tensor(out=wroute[s][:, :, 0:NE1], in0=epick[s][:, :, :], scalar=0.25,
                                                    in1=wide(esum[s][:, 1, :], NE1), op0=ALU.mult, op1=ALU.mult))
                    if k < NU:
                        dve.wait_ge(h3_ready[s].sem, h3_ready[s].at(n, k + 1))
                        dve.wait_ge(tanh_ready[s].sem, tanh_ready[s].at(n, k + 1))
                        if k >= 2:
                            dve.wait_ge(g_ready[s].sem, g_ready[s].at(n, k - 1))
                        V_.scalar_tensor_tensor(out=upT[s][:, k % 2, :], in0=tanhT[s][:, k % 2, :], scalar=1.0,
                                                in1=bank[:, S1[s], :], op0=ALU.add, op1=ALU.mult)\
                            .then_inc(up_ready[s].sem, 1)
                    if k < 2:
                        largest(k, NE1, s)
                    if k == 1:
                        V_.tensor_tensor(score2[s][:, :, 0:NE1], sc, wide(top[s][:, 0, :], NE1), ALU.subtract)\
                            .then_inc(mshift_ready[s].sem, 1)
                    u = k - 2 if k == NU + 1 else k - 3
                    if u >= 0 and u % CH == CH - 1:
                        e = u // CH
                        dve.wait_ge(down_done[s].sem, down_done[s].at(n, u + 1))
                        for t in range(T):
                            if e:
                                dve.wait_ge(down_used[s].sem, down_used[s].at(n, (e - 1) * T + t + 1))
                            i = V_.scalar_tensor_tensor(out=X[s][:, t, :],
                                                        in0=bank[:, (Y1, Y0)[e % 2][s], t * P:(t + 1) * P],
                                                        scalar=wroute[s][:, t, e:e + 1], in1=X[s][:, t, :],
                                                        op0=ALU.mult, op1=ALU.add)
                            i.then_inc(down_used[s].sem, 1)
                    if k == NU + 1:
                        dve.wait_ge(down_used[s].sem, down_used[s].at(n, NE1 * T))
                    yield

            def pre(n, f, s):
                yield from front(f, s, X[s], True, True)
                dve.wait_ge(proj_ready[s].sem, proj_ready[s].at(n, 1))
                V_.tensor_tensor(rope_kb[s][:, :], bank[HK:2 * HK, Y0[s], :], cossink[HK:2 * HK, :], ALU.mult)
                V_.tensor_tensor(rope_ka[s][:, :], bank[0:HK, Y0[s], :], cossink[0:HK, :], ALU.mult)\
                    .then_inc(rope_mul[s].sem, 1)
                dve.wait_ge(rope_mul[s].sem, rope_mul[s].at(n, 1))
                V_.tensor_tensor(rope_ka[s][:, :], rope_ka[s][:, :], rope_kb[s][:, :], ALU.add).then_inc(rope_ready[s].sem, 1)
                dve.wait_ge(proj_ready[s].sem, proj_ready[s].at(n, 3))
                V_.tensor_tensor(rope_b[s][:, :], bank[:, S1[s], :], sinq[:, :], ALU.mult)
                V_.tensor_tensor(rope_a[s][:, :], bank[:, S0[s], :], cosq[:, :], ALU.mult).then_inc(rope_mul[s].sem, 1)
                dve.wait_ge(rope_mul[s].sem, rope_mul[s].at(n, 2))
                V_.tensor_tensor(rope_a[s][:, :], rope_a[s][:, :], rope_b[s][:, :], ALU.add).then_inc(rope_ready[s].sem, 1)
                yield
                kq = ((rope_ka, k_part, k_rest), (rope_a, q_part, q_rest))
                for c, (rope, part, rest) in enumerate(kq):
                    dve.wait_ge(part0_ready[s].sem, part0_ready[s].at(n, c + 1))
                    V_.tensor_tensor(rest[s][:, :], rope[s][:, :], part[s][:, 0, :], ALU.subtract).then_inc(rest_ready[s].sem, 1)
                yield
                for c, (rope, part, rest) in enumerate(kq):
                    dve.wait_ge(part1_ready[s].sem, part1_ready[s].at(n, c + 1))
                    V_.tensor_tensor(part[s][:, 2, :], rest[s][:, :], part[s][:, 1, :], ALU.subtract)\
                        .then_inc(part2_ready[s].sem, 1)
                dve.wait_ge(proj_ready[s].sem, proj_ready[s].at(n, 4))
                V_.tensor_copy(Vp[s][:, :, :, 0:HD],
                               bank[:, Y1[s], 0:T * HK].rearrange("p (t v d) -> p t v d", t=T, v=KV))\
                    .then_inc(v_ready[s].sem, 1)
                yield

            def heads(n, s):

                def mx_unit(g, u):
                    t, heads = MX_UNITS[u]
                    dve.wait_ge(mx_ready[s].sem, mx_ready[s].at(n, g * MXU + u + 1))
                    if u == 0 and g >= 2:
                        dve.wait_ge(nparts_ready[s].sem, nparts_ready[s].at(n, g - 1))
                    c, w = len(heads), (t + 1) * P
                    src = bank[:, ring_bank(("mx", (g, u)), s), 0:c * w].rearrange("p (j k) -> p j k", j=c)
                    V_.tensor_reduce(nmax[s][:, g % 2, heads[0]:heads[0] + c, t], src, AX_X, ALU.max,
                                     negate=True).then_inc(mx_used[s].sem, 1)

                def normalize(g):
                    dve.wait_ge(o_turned[s].sem, o_turned[s].at(n, g + 1))
                    o = bank[:, AV[s], :].rearrange("p (t j r) -> p t j r", t=T, j=REP)
                    own(V_.reciprocal(den[s][:, :, :], o[:, :, :, HD]))
                    i = V_.tensor_tensor(heads_out[s][:, :, g * REP:(g + 1) * REP, :], o[:, :, :, 0:HD],
                                         den[s][:, :, :].unsqueeze(3).to_broadcast([P, T, REP, HD]), ALU.mult)
                    i.then_inc(heads_ready[s].sem, 1)

                for k in range(HEADS):
                    if k in MX_AT:
                        mx_unit(*MX_AT[k])
                    if k in OTURN_AT:
                        normalize(OTURN_AT[k])
                    yield

            walk(ffn, attn0, linear, moe, pre, heads, dve, dve_own)


def _rope_tables(np, S, dims, heads):
    inv = (1.0 / 10000.0 ** (np.arange(0, dims, 2, dtype=np.float32) / np.float32(dims))).astype(np.float32)
    freqs = np.arange(S, dtype=np.float32)[:, None] * inv[None, :]
    emb = np.concatenate([freqs, freqs], axis=-1).T
    sign = np.where(np.arange(dims) < dims // 2, -1.0, 1.0).astype(np.float32)[:, None]
    return (np.repeat(np.cos(emb).astype(np.float32), heads, axis=0),
            np.repeat(np.sin(emb).astype(np.float32) * sign, heads, axis=0))


def kernel(**inputs):
    import numpy as np
    import concourse.bacc as bacc
    from concourse.bass_utils import run_bass_kernel_spmd

    H, KV, HD = 16, 4, 8
    x = inputs["L0_attn_x"]
    B, S, D = x.shape

    def by_dim(w, heads):
        return w.reshape(D, heads, HD).transpose(0, 2, 1).reshape(D, heads * HD)

    def swapped(w):
        return w.reshape(D, 2, -1)[:, ::-1, :].reshape(D, -1)

    W, b = inputs["L0_attn_W"], inputs["L0_attn_b"]
    wq, wk = by_dim(inputs["L1_ffn_wq"], H), by_dim(inputs["L1_ffn_wk"], KV)
    cosq, sinq = _rope_tables(np, S, HD, H)
    cosk, sink = _rope_tables(np, S, HD, KV)
    arrays = {
        "x": x, "W_gate": inputs["L0_ffn_W_gate"], "b_gate": inputs["L0_ffn_b_gate"],
        "W1": inputs["L0_ffn_W1"], "b1T": inputs["L0_ffn_b1"].T, "W2": inputs["L0_ffn_W2"],
        "b2": inputs["L0_ffn_b2"], "W": W, "bqk": b[0:2 * D].reshape(2, D).T, "bv": b[2 * D:],
        "WqT": inputs["L1_attn_Wq"].T, "WkT": inputs["L1_attn_Wk"].T, "WvT": inputs["L1_attn_Wv"].T,
        "P": inputs["L1_attn_P"], "g1": inputs["L1_ffn_g1"].reshape(D, 1), "g2": inputs["L1_ffn_g2"].reshape(D, 1),
        "wq": wq, "wq_swap": swapped(wq), "wk": wk, "wk_swap": swapped(wk), "wv": inputs["L1_ffn_wv"],
        "wo": inputs["L1_ffn_wo"], "gate": inputs["L1_ffn_gate"], "w1": inputs["L1_ffn_w1"],
        "w2": inputs["L1_ffn_w2"], "w3": inputs["L1_ffn_w3"],
        "ident": np.eye(D, dtype=np.float32),
        "causal": np.triu(np.full((D, D), MASKED, dtype=np.float32), 1),
        "cosq": cosq, "sinq": sinq, "cossink": np.concatenate([cosk, sink], axis=0),
        "rank": np.broadcast_to(np.arange(8, 0, -1, dtype=np.float32), (D, S // D, 8)),
    }
    nc = bacc.Bacc("TRN2", target_bir_lowering=False, num_devices=1)
    feed, ins = {}, {}
    for name, a in arrays.items():
        a = np.ascontiguousarray(a)
        feed[f"in_{name}"] = a
        ins[name] = nc.dram_tensor(f"in_{name}", a.shape, mybir.dt.from_np(a.dtype), kind="ExternalInput").ap()
    out = nc.dram_tensor("out_x", (B, S, D), F32, kind="ExternalOutput").ap()
    macaron_kernel(nc, ins, out)
    r = run_bass_kernel_spmd(nc, [feed], core_ids=[0])
    return r.results[0]["out_x"]
```
